# Optimizing a Trainium2 kernel written in Bass

```python
import numpy as np
import jax
import jax.numpy as jnp

def _softmax(x, axis=-1):
    return jax.nn.softmax(x, axis=axis)

def _gelu(x):
    return jax.nn.gelu(x, approximate=True)

def _silu(x):
    return jax.nn.silu(x)

def _sigmoid(x):
    return jax.nn.sigmoid(x)

def _layernorm(x, axis=-1, eps=1e-05):
    m = jnp.mean(x, axis=axis, keepdims=True)
    v = jnp.var(x, axis=axis, keepdims=True)
    return (x - m) / jnp.sqrt(v + eps)

def _scatter_add(tgt, idx, src, axis=0):
    return tgt.at[idx].add(src)

def _segment_sum(src, seg, n):
    return jax.ops.segment_sum(src, seg, n)
kernel_name = 'mk_gnn_resnorm_d4_gnn_r8_05caa0'

def setup_inputs(seed: int=0):
    np.random.seed(seed)
    _w = jnp.asarray

    def _rec_inputs():
        import jax
        import jax.numpy as jnp
        _gk = jax.random.key(seed)
        x = -0.0001006 + 1 * jax.random.normal(jax.random.fold_in(_gk, 1), (6250, 96), jnp.float32)
        src = jax.random.randint(jax.random.fold_in(_gk, 2), (200000,), 0, 6250, jnp.int32)
        dst = jnp.minimum((6250 * jax.random.uniform(jax.random.fold_in(_gk, 3), (200000,)) ** 2.0).astype(jnp.int32), 49999)
        _o = jnp.argsort(dst, stable=True)
        src = src[_o]
        dst = dst[_o]
        edge_attr_96 = 5.93493e-05 + 1.00006 * jax.random.normal(jax.random.fold_in(_gk, 12), (200000, 96), jnp.float32)
        return (x, src, dst, edge_attr_96)
    x, src, dst, edge_attr_96 = _rec_inputs()

    def _L0_gnn_setup():
        import jax, jax.numpy as jnp
        import numpy as np
        N, E = (6250, 100000)
        C_IN = 96
        HEADS, C_HEAD = (4, 24)
        NEG_SLOPE = 0.2
        LN_EPS = 1e-05
        key = jax.random.key(seed)
        ks = jax.random.split(key, 6)
        x = jax.random.normal(ks[0], (N, C_IN), dtype=jnp.float32)
        edge_index = jax.random.randint(ks[1], (2, E), 0, N, dtype=jnp.int32)
        W = jax.random.normal(ks[2], (C_IN, HEADS * C_HEAD), dtype=jnp.float32) / np.sqrt(C_IN)
        att_src = jax.random.normal(ks[3], (HEADS, C_HEAD), dtype=jnp.float32) / np.sqrt(C_HEAD)
        att_dst = jax.random.normal(ks[4], (HEADS, C_HEAD), dtype=jnp.float32) / np.sqrt(C_HEAD)
        bias = jnp.zeros((HEADS * C_HEAD,), dtype=jnp.float32)
        gamma = jnp.ones((HEADS * C_HEAD,), dtype=jnp.float32)
        beta = jnp.zeros((HEADS * C_HEAD,), dtype=jnp.float32)
        return {'x': x, 'edge_index': edge_index, 'W': W, 'att_src': att_src, 'att_dst': att_dst, 'bias': bias, 'gamma': gamma, 'beta': beta}
    _L0_gnn_all = _L0_gnn_setup()
    _L0_gnn_in = {k: v for k, v in _L0_gnn_all.items() if k in ('W', 'att_src', 'att_dst', 'bias', 'gamma', 'beta')}
    del _L0_gnn_all

    def _L1_gnn_setup():
        import jax, jax.numpy as jnp
        import numpy as np
        N_NODES = 6250
        N_EDGES = 100000
        D_IN = 96
        D_OUT = 96
        key = jax.random.key(seed)
        k1, k2, k3, k4 = jax.random.split(key, 4)
        feat = jax.random.normal(k1, (N_NODES, D_IN), dtype=jnp.float32)
        std = (2.0 / (D_IN + D_OUT)) ** 0.5
        weight = jax.random.normal(k2, (D_IN, D_OUT), dtype=jnp.float32) * std
        bias = jnp.zeros((D_OUT,), dtype=jnp.float32)
        src = jax.random.randint(k3, (N_EDGES,), 0, N_NODES, dtype=jnp.int64)
        dst = jax.random.randint(k4, (N_EDGES,), 0, N_NODES, dtype=jnp.int64)
        return {'feat': feat, 'weight': weight, 'bias': bias, 'src': src, 'dst': dst}
    _L1_gnn_all = _L1_gnn_setup()
    _L1_gnn_in = {k: v for k, v in _L1_gnn_all.items() if k in ('weight', 'bias')}
    del _L1_gnn_all

    def _L2_gnn_setup():
        import jax, jax.numpy as jnp
        import numpy as np
        N_NODES = 6250
        N_EDGES = 100000
        IN_DIM = 96
        NUM_HEADS = 8
        HEAD_DIM = IN_DIM // NUM_HEADS
        key = jax.random.key(seed)
        ks = jax.random.split(key, 11)
        s = 1.0 / np.sqrt(IN_DIM)
        return {'x': jax.random.normal(ks[0], (N_NODES, IN_DIM), dtype=jnp.float32), 'edge_index': jax.random.randint(ks[1], (2, N_EDGES), 0, N_NODES, dtype=jnp.int64), 'edge_attr': jax.random.normal(ks[2], (N_EDGES, IN_DIM), dtype=jnp.float32), 'Wq': jax.random.normal(ks[3], (IN_DIM, IN_DIM), dtype=jnp.float32) * s, 'bq': jax.random.normal(ks[4], (IN_DIM,), dtype=jnp.float32) * s, 'Wk': jax.random.normal(ks[5], (IN_DIM, IN_DIM), dtype=jnp.float32) * s, 'bk': jax.random.normal(ks[6], (IN_DIM,), dtype=jnp.float32) * s, 'We': jax.random.normal(ks[7], (IN_DIM, IN_DIM), dtype=jnp.float32) * s, 'be': jax.random.normal(ks[8], (IN_DIM,), dtype=jnp.float32) * s, 'Wv': jax.random.normal(ks[9], (IN_DIM, IN_DIM), dtype=jnp.float32) * s, 'bv': jax.random.normal(ks[10], (IN_DIM,), dtype=jnp.float32) * s}
    _L2_gnn_all = _L2_gnn_setup()
    _L2_gnn_in = {k: v for k, v in _L2_gnn_all.items() if k in ('Wq', 'bq', 'Wk', 'bk', 'We', 'be', 'Wv', 'bv')}
    del _L2_gnn_all

    def _L3_gnn_setup():
        import jax, jax.numpy as jnp
        import numpy as np
        N_NODES = 6250
        N_EDGES = 100000
        D = 96

        def _gcn_conv(x, row, col, W, b, n):
            loop = jnp.arange(n, dtype=row.dtype)
            r = jnp.concatenate([row, loop])
            c = jnp.concatenate([col, loop])
            w = jnp.ones(r.shape[0], dtype=x.dtype)
            deg = jax.ops.segment_sum(w, c, num_segments=n)
            dinv = jnp.where(deg > 0, jax.lax.rsqrt(deg), 0.0).astype(x.dtype)
            norm = dinv[r] * w * dinv[c]
            h = x @ W
            msg = h[r] * norm[:, None]
            out = jax.ops.segment_sum(msg, c, num_segments=n)
            return out + b
        key = jax.random.key(seed)
        k1, k2, k3, k4 = jax.random.split(key, 4)
        s = 1.0 / np.sqrt(D)
        return {'x': jax.random.normal(k1, (N_NODES, D), dtype=jnp.float32), 'edge_index': jax.random.randint(k2, (2, N_EDGES), 0, N_NODES, dtype=jnp.int64), 'W1': jax.random.normal(k3, (D, D), dtype=jnp.float32) * s, 'b1': jnp.zeros((D,), dtype=jnp.float32), 'W2': jax.random.normal(k4, (D, D), dtype=jnp.float32) * s, 'b2': jnp.zeros((D,), dtype=jnp.float32)}
    _L3_gnn_all = _L3_gnn_setup()
    _L3_gnn_in = {k: v for k, v in _L3_gnn_all.items() if k in ('W1', 'b1', 'W2', 'b2')}
    del _L3_gnn_all
    return {'x': x, 'src': src, 'dst': dst, 'edge_attr_96': edge_attr_96, 'L0_gnn_W': _L0_gnn_in['W'], 'L0_gnn_att_src': _L0_gnn_in['att_src'], 'L0_gnn_att_dst': _L0_gnn_in['att_dst'], 'L0_gnn_bias': _L0_gnn_in['bias'], 'L0_gnn_gamma': _L0_gnn_in['gamma'], 'L0_gnn_beta': _L0_gnn_in['beta'], 'L1_gnn_weight': _L1_gnn_in['weight'], 'L1_gnn_bias': _L1_gnn_in['bias'], 'L2_gnn_Wq': _L2_gnn_in['Wq'], 'L2_gnn_bq': _L2_gnn_in['bq'], 'L2_gnn_Wk': _L2_gnn_in['Wk'], 'L2_gnn_bk': _L2_gnn_in['bk'], 'L2_gnn_We': _L2_gnn_in['We'], 'L2_gnn_be': _L2_gnn_in['be'], 'L2_gnn_Wv': _L2_gnn_in['Wv'], 'L2_gnn_bv': _L2_gnn_in['bv'], 'L3_gnn_W1': _L3_gnn_in['W1'], 'L3_gnn_b1': _L3_gnn_in['b1'], 'L3_gnn_W2': _L3_gnn_in['W2'], 'L3_gnn_b2': _L3_gnn_in['b2']}

def reference(x, src, dst, edge_attr_96, L0_gnn_W, L0_gnn_att_src, L0_gnn_att_dst, L0_gnn_bias, L0_gnn_gamma, L0_gnn_beta, L1_gnn_weight, L1_gnn_bias, L2_gnn_Wq, L2_gnn_bq, L2_gnn_Wk, L2_gnn_bk, L2_gnn_We, L2_gnn_be, L2_gnn_Wv, L2_gnn_bv, L3_gnn_W1, L3_gnn_b1, L3_gnn_W2, L3_gnn_b2):
    import jax
    import jax.numpy as jnp

    def _L0_gnn_ref(x, edge_index, W, att_src, att_dst, bias, gamma, beta):
        import jax, jax.numpy as jnp
        import numpy as np
        N, E = (6250, 100000)
        C_IN = 96
        HEADS, C_HEAD = (4, 24)
        NEG_SLOPE = 0.2
        LN_EPS = 1e-05
        n = x.shape[0]
        loop = jnp.arange(n, dtype=edge_index.dtype)
        src = jnp.concatenate([edge_index[0], loop])
        dst = jnp.concatenate([edge_index[1], loop])
        h = (x @ W).reshape(n, HEADS, C_HEAD)
        a_src = jnp.einsum('nhc,hc->nh', h, att_src)
        a_dst = jnp.einsum('nhc,hc->nh', h, att_dst)
        e = a_src[src] + a_dst[dst]
        e = jnp.where(e > 0, e, NEG_SLOPE * e)
        m = jax.ops.segment_max(e, dst, num_segments=n)
        ex = jnp.exp(e - m[dst])
        s = jax.ops.segment_sum(ex, dst, num_segments=n)
        alpha = ex / (s[dst] + 1e-16)
        msg = h[src] * alpha[:, :, None]
        out = jax.ops.segment_sum(msg, dst, num_segments=n).reshape(n, HEADS * C_HEAD)
        out = out + bias
        out = out + x
        mu = out.mean(-1, keepdims=True)
        var = ((out - mu) ** 2).mean(-1, keepdims=True)
        out = (out - mu) * jax.lax.rsqrt(var + LN_EPS) * gamma + beta
        return jax.nn.relu(out)

    def _L1_gnn_ref(feat, weight, bias, src, dst):
        import jax, jax.numpy as jnp
        import numpy as np
        N_NODES = 6250
        N_EDGES = 100000
        D_IN = 96
        D_OUT = 96
        N = feat.shape[0]
        ones = jnp.ones(src.shape[0], dtype=feat.dtype)
        out_deg = jax.ops.segment_sum(ones, src, num_segments=N)
        in_deg = jax.ops.segment_sum(ones, dst, num_segments=N)
        ci = jnp.clip(out_deg, 1.0, None) ** (-0.5)
        cj = jnp.clip(in_deg, 1.0, None) ** (-0.5)
        msg = feat[src] * ci[src, None]
        agg = jax.ops.segment_sum(msg, dst, num_segments=N) * cj[:, None]
        h = jnp.where(in_deg[:, None] > 0, agg, feat)
        return jnp.matmul(h, weight) + bias

    def _L2_gnn_ref(x, edge_index, edge_attr, Wq, bq, Wk, bk, We, be, Wv, bv):
        import jax, jax.numpy as jnp
        import numpy as np
        N_NODES = 6250
        N_EDGES = 100000
        IN_DIM = 96
        NUM_HEADS = 8
        HEAD_DIM = IN_DIM // NUM_HEADS
        N = x.shape[0]
        H, D = (NUM_HEADS, HEAD_DIM)
        Q_h = (x @ Wq + bq).reshape(N, H, D)
        K_h = (x @ Wk + bk).reshape(N, H, D)
        V_h = (x @ Wv + bv).reshape(N, H, D)
        E = (edge_attr @ We + be).reshape(-1, H, D)
        src_idx = edge_index[0]
        dst_idx = edge_index[1]
        src = K_h[src_idx]
        dest = Q_h[dst_idx]
        score = src * dest / jnp.sqrt(jnp.asarray(D, x.dtype))
        score = score * E
        score = jnp.exp(jnp.clip(score.sum(-1, keepdims=True), -5.0, 5.0))
        msg = V_h[src_idx] * score
        wV = jax.ops.segment_sum(msg, dst_idx, num_segments=N)
        Z = jax.ops.segment_sum(score, dst_idx, num_segments=N)
        h_out = wV / (Z + 1e-06)
        return h_out.reshape(N, H * D)

    def _L3_gnn_ref(x, edge_index, W1, b1, W2, b2):
        import jax, jax.numpy as jnp
        import numpy as np
        N_NODES = 6250
        N_EDGES = 100000
        D = 96

        def _gcn_conv(x, row, col, W, b, n):
            loop = jnp.arange(n, dtype=row.dtype)
            r = jnp.concatenate([row, loop])
            c = jnp.concatenate([col, loop])
            w = jnp.ones(r.shape[0], dtype=x.dtype)
            deg = jax.ops.segment_sum(w, c, num_segments=n)
            dinv = jnp.where(deg > 0, jax.lax.rsqrt(deg), 0.0).astype(x.dtype)
            norm = dinv[r] * w * dinv[c]
            h = x @ W
            msg = h[r] * norm[:, None]
            out = jax.ops.segment_sum(msg, c, num_segments=n)
            return out + b
        row, col = (edge_index[0], edge_index[1])
        n = x.shape[0]
        h = _gcn_conv(x, row, col, W1, b1, n)
        h = jax.nn.relu(h)
        out = _gcn_conv(h, row, col, W2, b2, n)
        return out
    edge_index = jnp.stack([src, dst])
    x = _layernorm(x + _L0_gnn_ref(x, edge_index, L0_gnn_W, L0_gnn_att_src, L0_gnn_att_dst, L0_gnn_bias, L0_gnn_gamma, L0_gnn_beta), axis=-1)
    x = _layernorm(x + _L1_gnn_ref(x, L1_gnn_weight, L1_gnn_bias, src, dst), axis=-1)
    x = _layernorm(x + _L2_gnn_ref(x, edge_index, edge_attr_96, L2_gnn_Wq, L2_gnn_bq, L2_gnn_Wk, L2_gnn_bk, L2_gnn_We, L2_gnn_be, L2_gnn_Wv, L2_gnn_bv), axis=-1)
    x = _layernorm(x + _L3_gnn_ref(x, edge_index, L3_gnn_W1, L3_gnn_b1, L3_gnn_W2, L3_gnn_b2), axis=-1)
    return x

_drawn_inputs = setup_inputs


def setup_inputs(seed=0):
    import zlib

    import numpy as np

    out = dict(_drawn_inputs(seed))
    spreads = {'L0_gnn_bias': (0.0, 0.1),
     'L0_gnn_gamma': (1.0, 0.2),
     'L0_gnn_beta': (0.0, 0.1),
     'L1_gnn_bias': (0.0, 0.1),
     'L3_gnn_b1': (0.0, 0.1),
     'L3_gnn_b2': (0.0, 0.1)}
    factors = {}
    for name, (base, spread) in spreads.items():
        noise = np.random.default_rng([zlib.crc32(name.encode()), seed]).standard_normal(out[name].shape)
        drawn = base * np.exp(spread * noise) if base else spread * noise
        out[name] = jnp.asarray(drawn.astype(out[name].dtype))
    for name, factor in factors.items():
        out[name] = (out[name] * factor).astype(out[name].dtype)
    return out
```

```python
from contextlib import ExitStack

import concourse.bass as bass
from concourse import mybir

P = 128
NODES = 6250
EDGES = 200000
D = 96
NB = -(-NODES // P)
TAIL = NODES - (NB - 1) * P
GROUP = 4
GROUPS = 4
BODY = GROUP * GROUPS
EDGE_TILES = -(-EDGES // P)
STEPS = -(-(EDGE_TILES + NB - 1) // BODY) * BODY
ITERS = STEPS // BODY
TILES = STEPS - NB + 1
NSC = -(-STEPS // P)
PITCH = 104
H0, C0 = 4, 24
H2, C2 = 8, 12
T0 = D + H0
NO_NODE = 60000
PB = 7
PROJ_ITERS = NB // PB
TILE_ROWS = TILES // 16
BIG = 1000.0

F32 = mybir.dt.float32
BF16 = mybir.dt.bfloat16
I32 = mybir.dt.int32
ALU = mybir.AluOpType
ACT = mybir.ActivationFunctionType
AX = mybir.AxisListType.X
RMAX = bass.bass_isa.ReduceOp.max

VECTORS = ["L0_gnn_att_src", "L0_gnn_att_dst", "L0_gnn_bias", "L0_gnn_gamma", "L0_gnn_beta", "L1_gnn_bias",
           "L2_gnn_bq", "L2_gnn_bk", "L2_gnn_bv", "L3_gnn_b1", "L3_gnn_b2"]

assert TILES % 16 == 0 and PROJ_ITERS * PB == NB and TILES * P >= EDGES


def gnn_stack(nc, ins, out):
    with ExitStack() as ctx:
        def sb(name, shape, dt=F32):
            return ctx.enter_context(nc.sbuf_tensor(name, shape, dt))

        def sem(name):
            return ctx.enter_context(nc.semaphore(name))

        def sems(name, n):
            return [sem(f"{name}{i}") for i in range(n)]

        table = [nc.dram_tensor(f"table{i}", [NB * P, w], F32).ap() for i, w in enumerate([T0, D, 2 * D, D, D])]
        row_dram = nc.dram_tensor("row_dram", [2, NSC * P], I32).ap()

        xres = sb("xres", [P, NB, D])
        acc = sb("acc", [P, NB * PITCH])
        qt = sb("qt", [P, NB * PITCH])
        tab = sb("tab", [P, NB * 2 * D])
        tmp = sb("tmp", [P, NB, D])
        accv = acc[:, :].rearrange("p (w c) -> p w c", w=NB)
        qtv = qt[:, :].rearrange("p (w c) -> p w c", w=NB)
        tab96 = tab[:, 0:NB * D].rearrange("p (w c) -> p w c", w=NB)
        tab100 = tab[:, 0:NB * T0].rearrange("p (w c) -> p w c", w=NB)
        tab192 = tab[:, :].rearrange("p (w c) -> p w c", w=NB)
        node = sb("node", [P, 12, NB])
        heads = sb("heads", [P, 2, NB * H2])
        mean, var, std, rstd = (node[:, i, :] for i in range(4))
        in_deg, out_deg, ci, cj, dinv, lone, dtmp = (node[:, i, :] for i in range(4, 11))
        gmax = sb("gmax", [P, 2, H0])

        src_s = sb("src_s", [P, STEPS + BODY], I32)
        drel_s = sb("drel_s", [P, STEPS + BODY])
        lo_s = tab[:, NB * T0:NB * T0 + STEPS]
        hi_s = tab[:, NB * T0 + STEPS:NB * T0 + 2 * STEPS]
        wrow = sb("wrow", [1, STEPS + BODY], I32)
        erow = sb("erow", [1, STEPS + BODY], I32)
        assert NB * T0 + 2 * STEPS <= NB * 2 * D

        ident = sb("ident", [P, P])
        iota = sb("iota", [P, P])
        iota_hi = sb("iota_hi", [P, NB])
        ones = sb("ones", [P, P])
        zero_bf = sb("zero_bf", [P, P], BF16)
        eps = sb("eps", [P, 1])
        w0 = sb("w0", [D, D])
        w1 = sb("w1", [D, D])
        wqkv = sb("wqkv", [D, 3 * D])
        we = sb("we", [D + 1, D])
        w3a = sb("w3a", [D, D])
        w3b = sb("w3b", [D, D])
        vecs = sb("vecs", [P, len(VECTORS), D])
        vrow = {n: vecs[:, i, :] for i, n in enumerate(VECTORS)}

        idx = sb("idx", [P, GROUPS, GROUP], I32)
        dcol = sb("dcol", [P, GROUPS, GROUP])
        gath = sb("gath", [P, BODY, 2 * D])
        onehot = sb("onehot", [P, GROUPS, GROUP, P])
        onehot_t = sb("onehot_t", [P, GROUP, P])
        msg = sb("msg", [P, GROUPS, GROUP, PITCH])
        logit = sb("logit", [P, 2, GROUP, H2])
        src_lo = sb("src_lo", [P, 2, GROUP, P], BF16)
        src_hi = sb("src_hi", [P, 2, GROUP, NB], BF16)
        eattr = sb("eattr", [P, BODY, D])
        eattr_t = sb("eattr_t", [D + 1, GROUP, P])
        prod = sb("prod", [P, GROUP, D])
        staged = sb("staged", [P, PB, D])
        xt = sb("xt", [D, PB, P])

        ps = ctx.enter_context(nc.psum_tensor("ps", [P, 8, 512], F32))

        s_const = sem("s_const")
        s_load = sem("s_load")
        s_rows = sems("s_rows", 2)
        s_wrap = sem("s_wrap")
        s_steps = sem("s_steps")
        s_eidx = sem("s_eidx")
        s_setup_pe = sem("s_setup_pe")
        s_setup_dve = sem("s_setup_dve")
        s_ready = sem("s_ready")
        s_table = sem("s_table")
        s_gmax = sem("s_gmax")
        s_act = sem("s_act")
        s_out = sem("s_out")
        chain_dve = sem("chain_dve")
        idx_ready = sems("idx_ready", GROUPS)
        onehot_ready = sems("onehot_ready", GROUPS)
        gathered = sems("gathered", BODY)
        summed = sems("summed", GROUPS)
        added = sems("added", GROUPS)
        turned = sems("turned", GROUPS)
        turned_sb = sems("turned_sb", GROUPS)
        spread = sems("spread", GROUPS)
        logits = sems("logits", GROUPS)
        exps = sems("exps", GROUPS)
        msgs = sems("msgs", GROUPS)
        histo = sems("histo", GROUPS)
        eloaded = sems("eloaded", BODY)
        eturned = sems("eturned", GROUPS)
        eturned_sb = sems("eturned_sb", GROUPS)
        dcol_ready = sems("dcol_ready", GROUPS)
        add_link = sems("add_link", BODY)
        link = [sems(f"link{q}_", 3) for q in range(GROUPS)]
        pool_step = sem("pool_step")
        proj_staged = sem("proj_staged")
        proj_turned = sems("proj_turned", 2)
        proj_sb = sems("proj_sb", 2)
        proj_done = sems("proj_done", PB)
        proj_out = sems("proj_out", PB)

        def bc(ap, n):
            return ap.unsqueeze(len(ap.shape)).broadcast_to(list(ap.shape) + [n])

        def mid(ap, n):
            return ap.unsqueeze(1).broadcast_to([ap.shape[0], n] + list(ap.shape[1:]))

        step_col = dtmp[:, 0:NSC]
        block_end = mean
        lmax = std[:, 0:16]
        tile_last = node[:, 11, :]
        advance = var
        wcol = rstd[:, 0:NSC]
        rows_cols = [heads[:, 0, 0:NSC].bitcast(I32), heads[:, 0, NSC:2 * NSC].bitcast(I32)]
        tile_idx = heads[:, 1, 0:NSC].bitcast(I32)
        ecol = heads[:, 1, NSC:2 * NSC]
        w128 = heads[:, 1, 2 * NSC:3 * NSC]
        cmp = tab[:, 0:NB * 49]
        steps_src = qt[:, 0:NSC * P].rearrange("p (c e) -> p c e", c=NSC).bitcast(I32)
        steps_dst = qt[:, NSC * P:2 * NSC * P].rearrange("p (c e) -> p c e", c=NSC).bitcast(I32)
        int_lo = acc[:, 0:NSC * P].rearrange("p (c e) -> p c e", c=NSC).bitcast(I32)
        int_hi = acc[:, NSC * P:2 * NSC * P].rearrange("p (c e) -> p c e", c=NSC).bitcast(I32)
        f_src, f_dst, f_lo, f_hi = (tab[:, i * NSC * P:(i + 1) * NSC * P].rearrange("p (c e) -> p c e", c=NSC) for i in range(4))
        f_lo = tmp[:, :, :].rearrange("p a b -> p (a b)")[:, 0:NSC * P].rearrange("p (c e) -> p c e", c=NSC)
        f_hi = tmp[:, :, :].rearrange("p a b -> p (a b)")[:, NSC * P:2 * NSC * P].rearrange("p (c e) -> p c e", c=NSC)
        f_pen = acc[:, 2 * NSC * P:3 * NSC * P].rearrange("p (c e) -> p c e", c=NSC)

        def load_blocks(engine, s):
            return nc.values_load_multi_w_load_instructions(
                wrow[0:1, bass.ds(s, GROUP)], engines=[engine], min_val=0, max_val=(NB - 1) * PITCH,
                skip_runtime_bounds_check_because="the setup writes at most (NB - 1) * PITCH")[1]

        block = ctx.enter_context(nc.Block())

        @block.sync
        def _(sp):
            xv = ins["x"][0:(NB - 1) * P, :].rearrange("(w p) c -> p w c", p=P)
            sp.wait_ge(s_const, 1)
            sp.dma_start(xres[:, 0:NB - 1, :], xv).then_inc(s_load, 16)
            sp.dma_start(xres[0:TAIL, NB - 1, :], ins["x"][(NB - 1) * P:, :]).then_inc(s_load, 16)
            sp.dma_start(tmp[0:TILE_ROWS, 0:16 * P // D + 1, :].rearrange("p a b -> p (a b)")[:, 0:16 * P].bitcast(I32),
                         ins["dst"].rearrange("(p t) -> p t", p=TILE_ROWS)).then_inc(s_load, 16)
            for t, n in ((w0, "L0_gnn_W"), (w1, "L1_gnn_weight"), (w3a, "L3_gnn_W1"), (w3b, "L3_gnn_W2")):
                sp.dma_start(t[:, :], ins[n]).then_inc(s_load, 16)
            for i, n in enumerate(("L2_gnn_Wq", "L2_gnn_Wk", "L2_gnn_Wv")):
                sp.dma_start(wqkv[:, i * D:(i + 1) * D], ins[n]).then_inc(s_load, 16)
            sp.dma_start(we[0:D, :], ins["L2_gnn_We"]).then_inc(s_load, 16)
            sp.dma_start(we[D:D + 1, :], ins["L2_gnn_be"].rearrange("(a c) -> a c", a=1)).then_inc(s_load, 16)
            for n in VECTORS:
                v = ins[n]
                v = v.rearrange("h c -> (h c)") if len(v.shape) == 2 else v
                sp.dma_start(vrow[n], v.partition_broadcast(P)).then_inc(s_load, 16)

            sp.wait_ge(s_eidx, 1)
            for i in range(2):
                sp.dma_start(row_dram[i, :].rearrange("(c p) -> p c", p=P), rows_cols[i],
                             allow_slow_non_contiguous=True).then_inc(s_rows[i], 16)
            for i, r in enumerate((wrow, erow)):
                sp.wait_ge(s_rows[i], 16)
                sp.dma_start(r[:, 0:STEPS], row_dram[i:i + 1, 0:STEPS]).then_inc(s_wrap, 16)
                sp.dma_start(r[:, STEPS:], row_dram[i:i + 1, 0:BODY]).then_inc(s_wrap, 16)

            def store_table(i, view):
                sp.wait_ge(s_ready, READY[f"table{i}"])
                sp.dma_start(table[i].rearrange("(w p) c -> p w c", p=P), view).then_inc(s_table, 16)

            store_table(0, tab100)
            store_table(1, tab96)
            store_table(2, tab192)
            sp.wait_ge(s_wrap, 64)

            def load_eattr(s, q):
                at = nc.values_load_multi_w_load_instructions(
                    erow[0:1, bass.ds(s + q * GROUP, GROUP)], engines=[mybir.EngineType.SP], min_val=0,
                    max_val=(TILES - 1) * P, skip_runtime_bounds_check_because="the setup writes at most (TILES - 1) * P")[1]
                for j in range(GROUP):
                    sp.dma_start(eattr[:, q * GROUP + j, :], ins["edge_attr_96"][bass.ds(at[j], P), :]).then_inc(
                        eloaded[q * GROUP + j], 16)

            for q in range(GROUPS):
                load_eattr(0, q)
            with sp.Fori(1, ITERS, 1) as k:
                for q in range(GROUPS):
                    sp.wait_ge(eturned[q], k)
                    load_eattr(k * BODY, q)
            store_table(3, tab96)
            store_table(4, tab96)
            sp.wait_ge(s_ready, READY["out"])
            sp.dma_start(out[0:(NB - 1) * P, :].rearrange("(w p) c -> p w c", p=P), xres[:, 0:NB - 1, :]).then_inc(s_out, 16)
            sp.dma_start(out[(NB - 1) * P:, :], xres[0:TAIL, NB - 1, :]).then_inc(s_out, 16)
            sp.wait_ge(s_table, 16 * 5)
            sp.wait_ge(s_out, 32)

        @block.gpsimd
        def _(pool):
            g = nc.gpsimd
            g.memset(xres[:, NB - 1, :], 0.0).then_inc(s_const, 1)
            g.memset(ones[:, :], 1.0).then_inc(s_const, 1)
            g.memset(zero_bf[:, :], 0.0).then_inc(s_const, 1)
            g.memset(eps[:, :], 1e-5).then_inc(s_const, 1)
            g.iota(iota[:, :], [[1, P]], base=0, channel_multiplier=0, allow_small_or_imprecise_dtypes=True).then_inc(s_const, 1)
            g.iota(iota_hi[:, :], [[1, NB]], base=0, channel_multiplier=0, allow_small_or_imprecise_dtypes=True).then_inc(s_const, 1)
            g.iota(step_col, [[P, NSC]], base=0, channel_multiplier=1, allow_small_or_imprecise_dtypes=True).then_inc(s_const, 1)
            g.iota(block_end, [[P, NB]], base=P, channel_multiplier=0, allow_small_or_imprecise_dtypes=True).then_inc(s_const, 1)
            pool.wait_ge(s_const, 8)
            g.affine_select(out=ident[:, :], in_=ones[:, :], compare_op=ALU.is_equal, fill=0.0, base=0,
                            pattern=[[-1, P]], channel_multiplier=1).then_inc(s_const, 1)
            pool.wait_ge(s_eidx, 1)
            for c in range(NSC):
                for arr, n in ((steps_src, "src"), (steps_dst, "dst")):
                    pool.indirect_dma_start(arr[:, c, :], None, ins[n].rearrange("(t e) -> t e", e=P),
                                            bass.IndirectOffsetOnAxis(ap=tile_idx[:, c:c + 1], axis=0)).then_inc(s_steps, 16)
            pool.wait_ge(s_ready, READY["gmax"])
            g.partition_all_reduce(gmax[:, 1, :], gmax[:, 0, :], P, RMAX).then_inc(s_gmax, 1)

            def gather_pass(number, width):
                pool.wait_ge(s_table, 16 * (number + 1))
                with pool.Fori(number * ITERS, (number + 1) * ITERS, 1) as i:
                    for q in range(GROUPS):
                        pool.wait_ge(idx_ready[q], i + 1)
                        pool.sem_inc(pool_step, 1)
                        for j in range(GROUP):
                            slot = q * GROUP + j
                            pool.indirect_dma_start(
                                gath[:, slot, 0:width], None, table[number],
                                bass.IndirectOffsetOnAxis(ap=idx[:, q, j:j + 1], axis=0)).then_inc(gathered[slot], 16)

            for number, width in enumerate([T0, D, 2 * D, D, D][:PASSES]):
                gather_pass(number, width)

        @block.tensor
        def _(pe):
            mm = nc.tensor.matmul
            pe.wait_ge(s_const, 9)
            pe.wait_ge(s_setup_dve, 1)
            mm(ps[:, 0, 0:NB], ones[0:TILE_ROWS, :], tile_last[0:TILE_ROWS, :], start=True, stop=True).then_inc(s_setup_pe, 1)
            pe.wait_ge(s_setup_dve, 2)
            for k, arr in enumerate((f_src, f_dst, f_lo, f_hi)):
                for c in range(NSC):
                    n = k * NSC + c
                    if n >= 8:
                        pe.wait_ge(s_setup_dve, 2 + n - 7)
                    nc.tensor.transpose(ps[:, n % 8, 0:P], arr[:, c, :],
                                        ident[:, :]).then_inc(s_setup_pe, 1)

            def project(call, weights, width):
                with pe.Fori(call * PROJ_ITERS, (call + 1) * PROJ_ITERS, 1) as i:
                    pe.wait_ge(proj_staged, i + 1)
                    for half, blocks in enumerate((range(0, 4), range(4, PB))):
                        pe.wait_ge(proj_sb[half], i + 1)
                        for b in blocks:
                            t = nc.tensor.transpose(ps[0:D, half, b % 4 * P:b % 4 * P + P],
                                                    staged[:, b, :], ident[:, :])
                        t.then_inc(proj_turned[half], 1)
                    for b in range(PB):
                        if b % 4 == 0:
                            pe.wait_ge(proj_sb[b // 4], i + 2)
                        pe.wait_ge(proj_out[b], i + 1)
                        if b == 0:
                            pe.wait_ge(proj_out[PB - 1], i + 1)
                        if b == PB - 1:
                            pe.wait_ge(proj_out[0], i + 2)
                        mm(ps[:, 2 + b % 6, 0:width], xt[:, b, :], weights[:, 0:width],
                           start=True, stop=True).then_inc(proj_done[b], 1)

            def block_regs(s):
                return load_blocks(mybir.EngineType.PE, s)

            def turn(q, i, j):
                pe.wait_ge(onehot_ready[q], i + 1)
                for t in range(GROUP):
                    m = nc.tensor.transpose(ps[:, 0, t * P:t * P + P], onehot[:, q, t, :], ident[:, :])
                m.then_inc(turned[q], 1)

            def sums(q, width, source):
                for t in range(GROUP):
                    m = mm(ps[:, 6 + q % 2, t * PITCH:t * PITCH + width], onehot[:, q, t, :], source(t),
                           start=True, stop=True)
                m.then_inc(summed[q], 1)

            project(0, w0, D)
            pe.wait_ge(s_wrap, 64)
            pe.wait_ge(s_ready, READY["pass0"])
            mm(ps[:, 2, 0:NB], zero_bf[:, :], zero_bf[:, 0:NB], start=True, stop=False, skip_group_check=True)

            def spread0(q, i):
                w = block_regs(i * BODY + q * GROUP)
                pe.wait_ge(turned_sb[q], i + 1)
                for t in range(GROUP):
                    at = (q % 2 * GROUP + t) * 2 * H0
                    m = mm(ps[:, 1, at:at + 2 * H0], onehot_t[:, t, :], qt[:, bass.ds(w[t], 2 * H0)], start=True, stop=True)
                m.then_inc(spread[q], 1)

            def sum0(q, i):
                pe.wait_ge(histo[q], i + 1)
                for t in range(GROUP):
                    mm(ps[:, 2, 0:NB], src_lo[:, q % 2, t, :], src_hi[:, q % 2, t, :], start=False, stop=False,
                       skip_group_check=True)
                pe.wait_ge(msgs[q], i + 1)
                sums(q, D + H0 + 1, lambda t: msg[:, q, t, 0:D + H0 + 1])

            with pe.Fori(0, ITERS, 1) as i:
                for q in range(GROUPS):
                    turn(q, i, i)
                    if q:
                        sum0(q - 1, i)
                    spread0(q, i)
                sum0(GROUPS - 1, i)
            mm(ps[:, 2, 0:NB], zero_bf[:, :], zero_bf[:, 0:NB], start=False, stop=True,
               skip_group_check=True).then_inc(s_setup_pe, 1)

            def linear_pass(number):
                with pe.Fori(number * ITERS, (number + 1) * ITERS, 1) as i:
                    g = pe.snap(i * 16 + 16)
                    for q in range(GROUPS):
                        pe.wait_ge(onehot_ready[q], i + 1)
                        pe.wait_ge(added[(q + 2) % GROUPS], i + 1)
                        for t in range(GROUP):
                            pe.wait_ge(gathered[q * GROUP + t], g)
                            m = mm(ps[:, 6 + q % 2, t * PITCH:t * PITCH + D], onehot[:, q, t, :],
                                   gath[:, q * GROUP + t, 0:D], start=True, stop=True)
                        m.then_inc(summed[q], 1)

            if PASSES > 1:
                linear_pass(1)
                project(1, w1, D)

            def turn_eattr(q, k):
                for t in range(GROUP):
                    pe.wait_ge(eloaded[q * GROUP + t], k * 16 + 16)
                    m = nc.tensor.transpose(ps[0:D, 1, t * P:t * P + P], eattr[:, q * GROUP + t, :], ident[:, :])
                m.then_inc(eturned[q], 1)

            def spread2(q, j, k):
                w = block_regs(k * BODY + q * GROUP)
                pe.wait_ge(turned_sb[q], j + 1)
                for t in range(GROUP):
                    mm(ps[:, 2 + q % 2, t * D:(t + 1) * D], onehot_t[:, t, :], qt[:, bass.ds(w[t], D)], start=True, stop=True)
                pe.wait_ge(eturned_sb[q], k + 1)
                for t in range(GROUP):
                    m = mm(ps[:, 4 + q % 2, t * D:(t + 1) * D], eattr_t[:, t, :], we[:, :], start=True, stop=True)
                m.then_inc(spread[q], 1)

            def sum2(q, j):
                pe.wait_ge(msgs[q], j + 1)
                sums(q, D + H2, lambda t: msg[:, q, t, 0:D + H2])

            if PASSES > 2:
                project(2, wqkv, 3 * D)
                pe.wait_ge(s_ready, READY["pass2"])
                with pe.Fori(2 * ITERS, 3 * ITERS, 1) as i:
                    j = pe.snap(i - ITERS)
                    k = pe.snap(i - 2 * ITERS)
                    for q in range(GROUPS):
                        turn(q, i, j)
                        turn_eattr(q, k)
                        if q:
                            sum2(q - 1, j)
                        spread2(q, j, k)
                    sum2(GROUPS - 1, j)
            if PASSES > 3:
                project(3, w3a, D)
                linear_pass(3)
                project(4, w3b, D)
                linear_pass(4)

        @block.scalar
        def _(act):
            for s in proj_sb:
                act.sem_inc(s, 1)
            act.wait_ge(s_const, 9)

            def project(call):
                act.wait_ge(s_ready, READY[f"project{call}"])
                source = (xres, tmp, xres, xres, tmp)[call][:, :, :].rearrange("p w c -> p (w c)")
                with act.Fori(call * PROJ_ITERS, (call + 1) * PROJ_ITERS, 1) as i:
                    nc.scalar.activation(staged[:, :, :].rearrange("p b c -> p (b c)"),
                                         source[:, bass.ds((i - call * PROJ_ITERS) * PB * D, PB * D)],
                                         ACT.Copy).then_inc(proj_staged, 1)
                    for half, (a, b) in enumerate(((0, 4), (4, PB))):
                        act.wait_ge(proj_turned[half], i + 1)
                        nc.scalar.activation(xt[:, a:b, :], ps[0:D, half, 0:(b - a) * P].rearrange("p (b c) -> p b c", c=P),
                                             ACT.Copy).then_inc(proj_sb[half], 1)

            def whole(need, out_, in_, func, **kw):
                act.wait_ge(s_ready, READY[need])
                nc.scalar.activation(out_, in_, func, **kw).then_inc(s_act, 1)

            def norm_roots(name):
                whole(f"{name}_sq", tab96, tmp[:, :, :], ACT.Square)
                whole(f"{name}_var", std, var, ACT.Sqrt, bias=eps[:, 0:1], scale=1.0 / D)

            def copy_turned(q, j):
                act.wait_ge(turned[q], j + 1)
                nc.scalar.activation(onehot_t[:, :, :], ps[:, 0, :].rearrange("p (j e) -> p j e", j=GROUP),
                                     ACT.Copy).then_inc(turned_sb[q], 1)

            def exp_logits(q, j, heads_):
                act.wait_ge(logits[q], j + 1)
                nc.scalar.activation(msg[:, q, :, D:D + heads_], logit[:, q % 2, :, 0:heads_], ACT.Exp).then_inc(exps[q], 1)

            project(0)
            whole("self", accv[:, :, D:D + H0], accv[:, :, D:D + H0], ACT.Exp)
            with act.Fori(0, ITERS, 1) as i:
                for q in range(GROUPS):
                    copy_turned(q, i)
                    exp_logits(q, i, H0)
            norm_roots("n0")
            norm_roots("n1")
            whole("roots", node[:, 6:9, :], node[:, 6:9, :], ACT.Sqrt)
            if PASSES > 1:
                project(1)
                norm_roots("n2")
            if PASSES > 2:
                project(2)
                with act.Fori(ITERS, 2 * ITERS, 1) as j:
                    k = act.snap(j - ITERS)
                    for q in range(GROUPS):
                        copy_turned(q, j)
                        act.wait_ge(eturned[q], k + 1)
                        nc.scalar.activation(eattr_t[0:D, :, :], ps[0:D, 1, :].rearrange("p (j e) -> p j e", j=GROUP),
                                             ACT.Copy).then_inc(eturned_sb[q], 1)
                        exp_logits(q, j, H2)
                norm_roots("n3")
            if PASSES > 3:
                project(3)
                project(4)
                norm_roots("n4")

        @block.vector
        def _(dve):
            v = nc.vector
            links = [0]
            told = [0]

            def chain(ins):
                links[0] += 1
                ins.then_inc(chain_dve, 1)
                dve.wait_ge(chain_dve, links[0])

            def ready(name):
                told[0] += 1
                assert READY[name] == told[0], name
                dve.sem_inc(s_ready, 1)

            def await_act(name):
                dve.wait_ge(s_act, ACT_DONE[name])

            def refill(q, i, s):
                v.tensor_copy(idx[:, q, :], src_s[:, bass.ds(s, GROUP)]).then_inc(idx_ready[q], 1)
                v.tensor_copy(dcol[:, q, :], drel_s[:, bass.ds(s, GROUP)]).then_inc(dcol_ready[q], 1)
                dve.wait_ge(dcol_ready[q], i)
                for t in range(GROUP):
                    o = v.tensor_scalar(onehot[:, q, t, :], iota[:, :], dcol[:, q, t:t + 1], None, ALU.is_equal)
                o.then_inc(onehot_ready[q], 1)

            def add_sums(q, i, s, width):
                w = load_blocks(mybir.EngineType.DVE, s)
                dve.wait_ge(summed[q], i + 1)
                for t in range(GROUP):
                    if t:
                        dve.wait_ge(add_link[q * GROUP + t], i + 1)
                    elif q:
                        dve.wait_ge(added[q - 1], i + (1 if q - 1 < 2 else 2))
                    else:
                        dve.wait_ge(added[GROUPS - 1], i + 1)
                    a = v.tensor_tensor(acc[:, bass.ds(w[t], width)], acc[:, bass.ds(w[t], width)],
                                        ps[:, 6 + q % 2, t * PITCH:t * PITCH + width], ALU.add)
                    a.then_inc(added[q] if t == GROUP - 1 else add_link[q * GROUP + t + 1], 1)

            def next_columns(i, last):
                return dve.snap((i - last * ITERS + 1) * BODY)

            def project(call, stores):
                with dve.Fori(call * PROJ_ITERS, (call + 1) * PROJ_ITERS, 1) as i:
                    first = dve.snap(i * PB - call * NB)
                    for b in range(PB):
                        dve.wait_ge(proj_done[b], i + 1)
                        for n, (dst, pitch, a, z) in enumerate(stores):
                            c = v.tensor_copy(dst[:, bass.ds((first + b) * pitch, z - a)], ps[:, 2 + b % 6, a:z])
                        c.then_inc(proj_out[b], 1)
                for b in range(PB):
                    dve.wait_ge(proj_out[b], (call + 1) * PROJ_ITERS + 1)

            def norm(name, src, dst):
                chain(v.tensor_reduce(mean, src, AX, ALU.add))
                chain(v.tensor_scalar(mean, mean, 1.0 / D, None, ALU.mult))
                chain(v.tensor_tensor(tmp[:, :, :], src, bc(mean, D), ALU.subtract))
                ready(f"{name}_sq")
                await_act(f"{name}_sq")
                chain(v.tensor_reduce(var, tab96, AX, ALU.add))
                ready(f"{name}_var")
                await_act(f"{name}_var")
                chain(v.reciprocal(rstd, std))
                chain(v.tensor_tensor(dst, tmp[:, :, :], bc(rstd, D), ALU.mult))

            for s in (added[2], added[3], *proj_out):
                dve.sem_inc(s, 1)
            dve.wait_ge(s_const, 9)
            dve.wait_ge(s_load, 16 * LOADS)
            R = TILE_ROWS
            edge_dst = tmp[0:R, :, :].rearrange("p a b -> p (a b)")[:, 0:16 * P].bitcast(I32)
            chain(v.tensor_reduce(lmax[0:R, :], edge_dst.rearrange("p (t e) -> p t e", e=P), AX, ALU.max))
            over = cmp[0:R, 0:NB * 16].rearrange("p (w t) -> p w t", w=NB)
            chain(v.tensor_tensor(over, mid(lmax[0:R, :], NB), bc(block_end[0:R, :], 16), ALU.is_lt))
            chain(v.tensor_reduce(tile_last[0:R, :], over, AX, ALU.add))
            dve.sem_inc(s_setup_dve, 1)
            dve.wait_ge(s_setup_pe, 1)
            chain(v.tensor_tensor(advance, ps[:, 0, 0:NB], iota_hi[:, :], ALU.add))
            past = cmp[:, 0:NSC * (NB - 1)].rearrange("p (c w) -> p c w", c=NSC)
            chain(v.tensor_tensor(past, mid(advance[:, 0:NB - 1], NSC), bc(step_col, NB - 1), ALU.is_lt))
            chain(v.tensor_reduce(wcol, past, AX, ALU.add))
            chain(v.tensor_tensor(ecol, step_col, wcol, ALU.subtract))
            chain(v.tensor_scalar(ecol, ecol, float(TILES - 1), None, ALU.min))
            chain(v.tensor_copy(tile_idx, ecol))
            chain(v.tensor_scalar(rows_cols[0], wcol, float(PITCH), None, ALU.mult))
            chain(v.tensor_scalar(rows_cols[1], ecol, float(P), None, ALU.mult))
            chain(v.tensor_scalar(w128, wcol, float(P), None, ALU.mult))
            dve.sem_inc(s_eidx, 1)
            dve.wait_ge(s_steps, 16 * 2 * NSC)
            chain(v.tensor_copy(f_src, steps_src))
            chain(v.tensor_copy(f_dst, steps_dst))
            chain(v.tensor_tensor(f_dst, f_dst, bc(w128, P), ALU.subtract))
            chain(v.tensor_scalar(int_lo, steps_src, P - 1, None, ALU.bitwise_and))
            chain(v.tensor_scalar(int_hi, steps_src, P.bit_length() - 1, None, ALU.logical_shift_right))
            chain(v.tensor_copy(f_lo, int_lo))
            chain(v.tensor_copy(f_hi, int_hi))
            chain(v.tensor_scalar(f_pen, f_dst, 0.0, BIG, ALU.is_lt, ALU.mult))
            chain(v.tensor_tensor(f_hi, f_hi, f_pen, ALU.add))
            chain(v.tensor_scalar(f_pen, f_dst, float(P), BIG, ALU.is_ge, ALU.mult))
            chain(v.tensor_tensor(f_hi, f_hi, f_pen, ALU.add))
            dve.sem_inc(s_setup_dve, 1)
            for k, dst in enumerate((src_s, drel_s, lo_s, hi_s)):
                for c in range(NSC):
                    n = k * NSC + c
                    m = min(P, STEPS - c * P)
                    dve.wait_ge(s_setup_pe, 2 + n)
                    v.tensor_copy(dst[:, c * P:c * P + m], ps[:, n % 8, 0:m]).then_inc(s_setup_dve, 1)
            dve.wait_ge(s_setup_dve, 2 + 4 * NSC)
            chain(v.tensor_copy(src_s[:, STEPS:], src_s[:, 0:BODY]))
            chain(v.tensor_copy(drel_s[:, STEPS:], drel_s[:, 0:BODY]))
            chain(v.memset(eattr_t[D:D + 1, :, :], 1.0))
            chain(v.memset(msg[:, :, :, D + H0:D + H0 + 1], 1.0))
            for q in range(GROUPS):
                refill(q, 1, q * GROUP)
            dve.wait_ge(s_wrap, 64)

            ready("project0")
            project(0, [(tab, T0, 0, D)])
            htab = tab100[:, :, 0:D]
            a_src, a_dst, guard = tab100[:, :, D:D + H0], qtv[:, :, 0:H0], qtv[:, :, H0:2 * H0]
            by_head = tmp[:, :, :].rearrange("p w (h c) -> p w h c", h=H0)
            hv = heads[:, 0, 0:NB * H0].rearrange("p (w h) -> p w h", w=NB)
            ex_self = accv[:, :, D:D + H0]
            for att, to in (("L0_gnn_att_src", a_src), ("L0_gnn_att_dst", a_dst)):
                chain(v.tensor_tensor(tmp[:, :, :], htab, mid(vrow[att], NB), ALU.mult))
                chain(v.tensor_reduce(to, by_head, AX, ALU.add))
            chain(v.tensor_reduce(gmax[:, 0, :], a_src.rearrange("p w h -> p h w"), AX, ALU.max))
            ready("table0")
            ready("gmax")
            dve.wait_ge(s_gmax, 1)
            chain(v.tensor_tensor(hv, a_dst, mid(gmax[:, 1, :], NB), ALU.add))
            chain(v.scalar_tensor_tensor(out=guard, in0=hv, scalar=0.2, in1=hv, op0=ALU.mult, op1=ALU.max))
            chain(v.tensor_tensor(hv, a_src, a_dst, ALU.add))
            chain(v.scalar_tensor_tensor(out=hv, in0=hv, scalar=0.2, in1=hv, op0=ALU.mult, op1=ALU.max))
            chain(v.tensor_tensor(hv, hv, guard, ALU.subtract))
            chain(v.tensor_scalar(ex_self, hv, 0.0, None, ALU.min))
            ready("self")
            await_act("self")
            chain(v.tensor_tensor(accv[:, :, 0:D].rearrange("p w (h c) -> p w h c", h=H0),
                                  htab.rearrange("p w (h c) -> p w h c", h=H0), bc(ex_self, C0), ALU.mult))
            chain(v.memset(accv[:, :, D + H0:D + H0 + 1], 0.0))
            ready("pass0")

            def logits0(q, i, g):
                for t in range(GROUP):
                    dve.wait_ge(gathered[q * GROUP + t], g)
                dve.wait_ge(spread[q], i + 1)
                at = q % 2 * GROUP * 2 * H0
                there = ps[:, 1, at:at + GROUP * 2 * H0].rearrange("p (j c) -> p j c", j=GROUP)
                lg = logit[:, q % 2, :, 0:H0]
                v.tensor_tensor(lg, gath[:, q * GROUP:(q + 1) * GROUP, D:D + H0], there[:, :, 0:H0], ALU.add).then_inc(link[q][0], 1)
                dve.wait_ge(link[q][0], i + 1)
                v.scalar_tensor_tensor(out=lg, in0=lg, scalar=0.2, in1=lg, op0=ALU.mult, op1=ALU.max).then_inc(link[q][1], 1)
                dve.wait_ge(link[q][1], i + 1)
                v.tensor_tensor(lg, lg, there[:, :, H0:2 * H0], ALU.subtract).then_inc(link[q][2], 1)
                dve.wait_ge(link[q][2], i + 1)
                v.tensor_scalar(lg, lg, 0.0, None, ALU.min).then_inc(logits[q], 1)

            def histo0(q, i):
                for t in range(GROUP):
                    v.tensor_scalar(src_lo[:, q % 2, t, :], iota[:, :], lo_s[:, bass.ds(i * BODY + q * GROUP + t, 1)], None, ALU.is_equal)
                v.tensor_tensor(src_hi[:, q % 2, :, :], mid(iota_hi[:, :], GROUP),
                                bc(hi_s[:, bass.ds(i * BODY + q * GROUP, GROUP)], NB), ALU.is_equal).then_inc(histo[q], 1)

            def messages(q, j, h, c, at):
                dve.wait_ge(exps[q], j + 1)
                v.tensor_tensor(msg[:, q, :, 0:D].rearrange("p j (h c) -> p j h c", h=h),
                                gath[:, q * GROUP:(q + 1) * GROUP, at:at + D].rearrange("p j (h c) -> p j h c", h=h),
                                bc(msg[:, q, :, D:D + h], c), ALU.mult).then_inc(msgs[q], 1)

            with dve.Fori(0, ITERS, 1) as i:
                g = dve.snap(i * 16 + 16)
                nxt = dve.snap((i + 1) * BODY)
                for q in range(GROUPS):
                    logits0(q, i, g)
                    histo0(q, i)
                    messages(q, i, H0, C0, 0)
                    if q:
                        add_sums(q - 1, i, i * BODY + (q - 1) * GROUP, D + H0 + 1)
                        refill(q - 1, i + 2, nxt + (q - 1) * GROUP)
                q = GROUPS - 1
                add_sums(q, i, i * BODY + q * GROUP, D + H0 + 1)
                refill(q, i + 2, nxt + q * GROUP)

            def pass_done(number):
                dve.wait_ge(added[GROUPS - 1], (number + 1) * ITERS + 1)

            pass_done(0)
            chain(v.tensor_scalar(hv, ex_self, 1e-16, None, ALU.add))
            chain(v.reciprocal(hv, hv))
            chain(v.tensor_tensor(by_head, accv[:, :, 0:D].rearrange("p w (h c) -> p w h c", h=H0), bc(hv, C0), ALU.mult))
            chain(v.tensor_tensor(tmp[:, :, :], tmp[:, :, :], mid(vrow["L0_gnn_bias"], NB), ALU.add))
            chain(v.tensor_tensor(tmp[:, :, :], tmp[:, :, :], xres[:, :, :], ALU.add))
            norm("n0", tmp[:, :, :], tmp[:, :, :])
            chain(v.tensor_tensor(tmp[:, :, :], tmp[:, :, :], mid(vrow["L0_gnn_gamma"], NB), ALU.mult))
            chain(v.tensor_tensor(tmp[:, :, :], tmp[:, :, :], mid(vrow["L0_gnn_beta"], NB), ALU.add))
            chain(v.scalar_tensor_tensor(out=xres[:, :, :], in0=tmp[:, :, :], scalar=0.0, in1=xres[:, :, :], op0=ALU.max, op1=ALU.add))
            norm("n1", xres[:, :, :], xres[:, :, :])
            dve.wait_ge(s_setup_pe, 2 + 4 * NSC)
            chain(v.tensor_copy(in_deg, accv[:, :, D + H0]))
            chain(v.tensor_copy(out_deg, ps[:, 2, 0:NB]))
            chain(v.tensor_scalar(ci, out_deg, 1.0, None, ALU.max))
            chain(v.tensor_scalar(cj, in_deg, 1.0, None, ALU.max))
            chain(v.tensor_scalar(dinv, in_deg, 1.0, None, ALU.add))
            chain(v.tensor_scalar(lone, in_deg, 0.0, None, ALU.is_equal))
            ready("roots")
            await_act("roots")
            chain(v.reciprocal(node[:, 6:9, :], node[:, 6:9, :]))

            def linear_pass(number):
                with dve.Fori(number * ITERS, (number + 1) * ITERS, 1) as i:
                    now = dve.snap((i - number * ITERS) * BODY)
                    nxt = dve.snap(now + BODY)
                    for q in range(GROUPS):
                        add_sums(q, i, now + q * GROUP, D)
                        refill(q, i + 2, nxt + q * GROUP)
                pass_done(number)

            if PASSES > 1:
                chain(v.tensor_tensor(tab96, xres[:, :, :], bc(ci, D), ALU.mult))
                ready("table1")
                chain(v.memset(acc[:, :], 0.0))
                linear_pass(1)
                chain(v.tensor_tensor(tmp[:, :, :], accv[:, :, 0:D], bc(cj, D), ALU.mult))
                chain(v.tensor_tensor(tab96, xres[:, :, :], bc(lone, D), ALU.mult))
                chain(v.tensor_tensor(tmp[:, :, :], tmp[:, :, :], tab96, ALU.add))
                ready("project1")
                project(1, [(tab, D, 0, D)])
                chain(v.tensor_tensor(xres[:, :, :], xres[:, :, :], mid(vrow["L1_gnn_bias"], NB), ALU.add))
                chain(v.tensor_tensor(xres[:, :, :], xres[:, :, :], tab96, ALU.add))
                norm("n2", xres[:, :, :], xres[:, :, :])

            if PASSES > 2:
                ready("project2")
                project(2, [(qt, PITCH, 0, D), (tab, 2 * D, D, 3 * D)])
                chain(v.tensor_tensor(tab192[:, :, 0:D], tab192[:, :, 0:D], mid(vrow["L2_gnn_bk"], NB), ALU.add))
                chain(v.tensor_tensor(tab192[:, :, D:], tab192[:, :, D:], mid(vrow["L2_gnn_bv"], NB), ALU.add))
                ready("table2")
                chain(v.tensor_tensor(qtv[:, :, 0:D], qtv[:, :, 0:D], mid(vrow["L2_gnn_bq"], NB), ALU.add))
                chain(v.tensor_scalar(qtv[:, :, 0:D], qtv[:, :, 0:D], float(C2) ** -0.5, None, ALU.mult))
                chain(v.memset(acc[:, :], 0.0))
                ready("pass2")

                def logits2(q, j, g):
                    for t in range(GROUP):
                        dve.wait_ge(gathered[q * GROUP + t], g)
                    dve.wait_ge(spread[q], j + 1)
                    view = lambda bank: ps[:, bank, 0:GROUP * D].rearrange("p (j c) -> p j c", j=GROUP)
                    v.tensor_tensor(prod[:, :, :], gath[:, q * GROUP:(q + 1) * GROUP, 0:D], view(2 + q % 2), ALU.mult).then_inc(link[q][0], 1)
                    dve.wait_ge(link[q][0], j + 1)
                    v.tensor_tensor(prod[:, :, :], prod[:, :, :], view(4 + q % 2), ALU.mult).then_inc(link[q][1], 1)
                    dve.wait_ge(link[q][1], j + 1)
                    lg = logit[:, q % 2, :, 0:H2]
                    v.tensor_reduce(lg, prod[:, :, :].rearrange("p j (h c) -> p j h c", h=H2), AX, ALU.add).then_inc(link[q][2], 1)
                    dve.wait_ge(link[q][2], j + 1)
                    v.tensor_scalar(lg, lg, 5.0, -5.0, ALU.min, ALU.max).then_inc(logits[q], 1)

                with dve.Fori(2 * ITERS, 3 * ITERS, 1) as i:
                    j = dve.snap(i - ITERS)
                    g = dve.snap(i * 16 + 16)
                    now = dve.snap((i - 2 * ITERS) * BODY)
                    nxt = dve.snap(now + BODY)
                    for q in range(GROUPS):
                        logits2(q, j, g)
                        messages(q, j, H2, C2, D)
                        if q:
                            add_sums(q - 1, i, now + (q - 1) * GROUP, D + H2)
                            refill(q - 1, i + 2, nxt + (q - 1) * GROUP)
                    q = GROUPS - 1
                    add_sums(q, i, now + q * GROUP, D + H2)
                    refill(q, i + 2, nxt + q * GROUP)
                pass_done(2)
                zv = heads[:, 0, 0:NB * H2].rearrange("p (w h) -> p w h", w=NB)
                by_head2 = tmp[:, :, :].rearrange("p w (h c) -> p w h c", h=H2)
                chain(v.tensor_scalar(zv, accv[:, :, D:D + H2], 1e-6, None, ALU.add))
                chain(v.reciprocal(zv, zv))
                chain(v.tensor_tensor(by_head2, accv[:, :, 0:D].rearrange("p w (h c) -> p w h c", h=H2), bc(zv, C2), ALU.mult))
                chain(v.tensor_tensor(xres[:, :, :], xres[:, :, :], tmp[:, :, :], ALU.add))
                norm("n3", xres[:, :, :], xres[:, :, :])

            if PASSES > 3:
                ready("project3")
                for number, bias in ((3, "L3_gnn_b1"), (4, "L3_gnn_b2")):
                    project(number, [(tab, D, 0, D)])
                    chain(v.tensor_tensor(tab96, tab96, bc(dinv, D), ALU.mult))
                    ready(f"table{number}")
                    chain(v.tensor_copy(accv[:, :, 0:D], tab96))
                    linear_pass(number)
                    chain(v.tensor_tensor(tmp[:, :, :], accv[:, :, 0:D], bc(dinv, D), ALU.mult))
                    chain(v.tensor_tensor(tmp[:, :, :], tmp[:, :, :], mid(vrow[bias], NB), ALU.add))
                    if number == 3:
                        chain(v.tensor_scalar(tmp[:, :, :], tmp[:, :, :], 0.0, None, ALU.max))
                        ready("project4")
                chain(v.tensor_tensor(xres[:, :, :], xres[:, :, :], tmp[:, :, :], ALU.add))
                norm("n4", xres[:, :, :], xres[:, :, :])
            ready("out")


PASSES = 5
LOADS = 12 + len(VECTORS)
_STAGES = [["project0", "table0", "gmax", "self", "pass0", "n0_sq", "n0_var", "n1_sq", "n1_var", "roots"],
           ["table1", "project1", "n2_sq", "n2_var"],
           ["project2", "table2", "pass2", "n3_sq", "n3_var"],
           ["project3", "table3", "project4", "table4", "n4_sq", "n4_var"], []]
READY = {n: i + 1 for i, n in enumerate([n for st in _STAGES[:PASSES] for n in st] + ["out"])}
ACT_DONE = {n: i + 1 for i, n in enumerate(n for n in READY if n in ("self", "roots") or n.endswith(("_sq", "_var")))}


EDGE_INS = {"src": 0, "dst": NO_NODE, "edge_attr_96": 0.0}


def kernel(**inputs):
    import numpy as _np
    import concourse.bacc as _bacc
    from concourse.bass_utils import run_bass_kernel_spmd as _run

    nc = _bacc.Bacc("TRN2", target_bir_lowering=False, num_devices=1)
    arrays, aps = {}, {}
    for name, a in inputs.items():
        a = _np.ascontiguousarray(a)
        if name in EDGE_INS:
            whole = _np.full((TILES * P,) + a.shape[1:], EDGE_INS[name], a.dtype)
            whole[:EDGES] = a
            a = whole
        arrays[f"in_{name}"] = a
        aps[name] = nc.dram_tensor(f"in_{name}", a.shape, mybir.dt.from_np(a.dtype), kind="ExternalInput").ap()
    out = nc.dram_tensor("out_x", (NODES, D), F32, kind="ExternalOutput").ap()
    gnn_stack(nc, aps, out)
    r = _run(nc, [arrays], core_ids=[0])
    return r.results[0]["out_x"]
```

```python
from contextlib import ExitStack

import concourse.bass as bass
from concourse import mybir

P = 128
NODES = 6250
EDGES = 200000
D = 96
NB = -(-NODES // P)
TAIL = NODES - (NB - 1) * P
GROUP = 4
GROUPS = 4
BODY = GROUP * GROUPS
EDGE_TILES = -(-EDGES // P)
STEPS = -(-(EDGE_TILES + NB - 1) // BODY) * BODY
ITERS = STEPS // BODY
TILES = STEPS
REACHED = STEPS - NB + 1
NSC = -(-STEPS // P)
PITCH = 104
H0, C0 = 4, 24
H2, C2 = 8, 12
PARTS0 = 3 * 2 * H0
T0 = D + H0
NO_NODE = 60000
PB = 7
PROJ_ITERS = NB // PB
TILE_ROWS = TILES // 16
E0, E1 = 1, GROUP - 1
BIG = 1000.0

F32 = mybir.dt.float32
BF16 = mybir.dt.bfloat16
I32 = mybir.dt.int32
ALU = mybir.AluOpType
ACT = mybir.ActivationFunctionType
AX = mybir.AxisListType.X
RMAX = bass.bass_isa.ReduceOp.max

VECTORS = ["L0_gnn_att_src", "L0_gnn_att_dst", "L0_gnn_bias", "L0_gnn_gamma", "L0_gnn_beta",
           "L3_gnn_b1", "L3_gnn_b2"]
HALVES = ((0, NB // 2 + 1), (NB // 2 + 1, NB))

assert TILES % 16 == 0 and PROJ_ITERS * PB == NB and TILES * P >= EDGES


def gnn_stack(nc, ins, out):
    with ExitStack() as ctx:
        def sb(name, shape, dt=F32):
            return ctx.enter_context(nc.sbuf_tensor(name, shape, dt))

        def sem(name):
            return ctx.enter_context(nc.semaphore(name))

        def sems(name, n):
            return [sem(f"{name}{i}") for i in range(n)]

        table = [nc.dram_tensor(f"table{i}", [NB * P, w], F32).ap() for i, w in enumerate([T0, D, 2 * D, D, D])]
        eproj = nc.dram_tensor("eproj", [TILES * P, D], F32).ap()
        row_dram = nc.dram_tensor("row_dram", [2, NSC * P], I32).ap()

        xres = sb("xres", [P, NB, D])
        acc = sb("acc", [P, NB * PITCH])
        qparts = [sb(f"qpart{i}", [P, NB * PITCH], BF16) for i in range(3)]
        qpart_v = [t[:, :].rearrange("p (w c) -> p w c", w=NB) for t in qparts]
        there = sb("there", [P, NB, 2 * H0])
        tab = sb("tab", [P, NB * 2 * D])
        tmp = sb("tmp", [P, NB, D])
        accv = acc[:, :].rearrange("p (w c) -> p w c", w=NB)
        tab96 = tab[:, 0:NB * D].rearrange("p (w c) -> p w c", w=NB)
        tab100 = tab[:, 0:NB * T0].rearrange("p (w c) -> p w c", w=NB)
        tab192 = tab[:, :].rearrange("p (w c) -> p w c", w=NB)
        node = sb("node", [P, 12, NB])
        heads = sb("heads", [P, 2, NB * H2])
        mean, var, std, rstd = (node[:, i, :] for i in range(4))
        in_deg, out_deg, ci, cj, dinv, lone, dtmp = (node[:, i, :] for i in range(4, 11))
        gmax = sb("gmax", [P, 2, H0])

        WORDS = 3
        steps = sb("steps", [P, STEPS + BODY, WORDS], I32)
        src_s = steps[:, :, 0]
        drel_s, lo_s, hi_s = (steps[:, :, :].bitcast(BF16)[:, :, c] for c in (2, 3, 4))
        rows = sb("rows", [2, STEPS + BODY], I32)
        wrow, erow = rows[0:1, :], rows[1:2, :]
        ident = sb("ident", [P, P])
        ident_bf = sb("ident_bf", [P, P], BF16)
        iota = sb("iota", [P, P], BF16)
        iota_hi = sb("iota_hi", [P, NB])
        ones = sb("ones", [P, P])
        zero_bf = sb("zero_bf", [P, P], BF16)
        eps = sb("eps", [P, 1])
        w0 = sb("w0", [D, D + 2 * H0])
        w1 = sb("w1", [D + 1, D])
        wqkv = sb("wqkv", [D + 1, 3 * D])
        we = sb("we", [D + 1, D])
        w3a = sb("w3a", [D, D])
        w3b = sb("w3b", [D, D])
        vecs = sb("vecs", [P, len(VECTORS), D])
        vrow = {n: vecs[:, i, :] for i, n in enumerate(VECTORS)}

        cols = sb("cols", [P, GROUPS, GROUP, WORDS], I32)
        dcol, locol, hicol = (cols[:, :, :, :].bitcast(BF16)[:, :, :, c] for c in (2, 3, 4))
        gath = sb("gath", [P, BODY, 2 * D])
        onehot = sb("onehot", [P, GROUPS, GROUP, P], BF16)
        onehot_f = sb("onehot_f", [P, GROUPS, GROUP, P])
        onehot_t = sb("onehot_t", [P, GROUP, P], BF16)
        msg = sb("msg", [P, GROUPS, GROUP, PITCH])
        dvals = sb("dvals", [P, 2, GROUP, 2 * H0])
        logit = sb("logit", [P, 2, GROUP, H2])
        eattr = sb("eattr", [P, BODY, D])
        at = [NB * T0]

        def behind(n):
            at[0] += n
            return tab[:, at[0] - n:at[0]]

        src_lo = behind(GROUP * P).bitcast(BF16).rearrange("p (r j e) -> p r j e", r=2, j=GROUP)
        src_hi = behind(GROUP * NB).bitcast(BF16).rearrange("p (r j e) -> p r j e", r=2, j=GROUP)
        eout = behind(GROUPS * E1 * D).rearrange("p (q j c) -> p q j c", q=GROUPS, j=E1)
        eattr_t = behind(E1 * P)[0:D + 1, :].rearrange("p (j e) -> p j e", j=E1)
        prod = tab[:, 0:GROUP * D].rearrange("p (j c) -> p j c", j=GROUP)
        flat = gath[:, :, :].rearrange("p s c -> p (s c)")
        staged = flat[:, 0:PB * D].rearrange("p (b c) -> p b c", b=PB)
        xt = flat[0:D + 1, PB * D:PB * (D + P)].rearrange("p (b c) -> p b c", b=PB)

        ps = ctx.enter_context(nc.psum_tensor("ps", [P, 8, 512], F32))

        s_const = sem("s_const")
        s_load_dst = sem("s_load_dst")
        s_load = sem("s_load")
        s_rows = sems("s_rows", 2)
        s_wrap = sem("s_wrap")
        s_steps = sem("s_steps")
        s_eidx = sem("s_eidx")
        s_setup_pe = sem("s_setup_pe")
        s_setup_dve = sem("s_setup_dve")
        s_ready = sem("s_ready")
        s_table = sem("s_table")
        s_gmax = sem("s_gmax")
        s_clear = sem("s_clear")
        s_act = sem("s_act")
        s_out = sem("s_out")
        chain_dve = sem("chain_dve")
        idx_ready = sems("idx_ready", GROUPS)
        onehot_ready = sems("onehot_ready", GROUPS)
        gathered = sems("gathered", GROUPS)
        summed = sems("summed", GROUPS)
        added = sems("added", GROUPS)
        turned = sems("turned", GROUPS)
        turned_sb = sems("turned_sb", GROUPS)
        spread = sems("spread", GROUPS)
        logits = sems("logits", GROUPS)
        exps = sems("exps", GROUPS)
        msgs = sems("msgs", GROUPS)
        histo = sems("histo", GROUPS)
        eloaded = sems("eloaded", GROUPS)
        onehot_f_ready = sems("onehot_f_ready", GROUPS)
        ein = sems("ein", GROUPS)
        eturned = sems("eturned", GROUPS)
        eturned_sb = sems("eturned_sb", GROUPS)
        eprojected = sems("eprojected", GROUPS)
        eout_ready = sems("eout_ready", GROUPS)
        estored = sems("estored", GROUPS)
        add_link = sems("add_link", BODY)
        link = [sems(f"link{q}_", 4) for q in range(GROUPS)]
        pool_step = sem("pool_step")
        proj_staged = sem("proj_staged")
        proj_turned = sems("proj_turned", 2)
        proj_sb = sems("proj_sb", 2)
        proj_done = sems("proj_done", PB)
        proj_out = sems("proj_out", PB)

        def bc(ap, n):
            return ap.unsqueeze(len(ap.shape)).broadcast_to(list(ap.shape) + [n])

        def mid(ap, n):
            return ap.unsqueeze(1).broadcast_to([ap.shape[0], n] + list(ap.shape[1:]))

        step_col = dtmp[:, 0:NSC]
        block_end = mean
        lmax = std[:, 0:16]
        tile_last = node[:, 11, :]
        advance = var
        wcol = rstd[:, 0:NSC]
        rows_cols = [heads[:, 0, 0:NSC].bitcast(I32), heads[:, 0, NSC:2 * NSC].bitcast(I32)]
        tile_idx = heads[:, 1, 0:NSC].bitcast(I32)
        ecol = heads[:, 1, NSC:2 * NSC]
        w128 = heads[:, 1, 2 * NSC:3 * NSC]
        cmp = tab[:, 0:NB * 49]
        steps_src, steps_dst = (tab[:, NB * T0 + i * NSC * P:NB * T0 + (i + 1) * NSC * P].rearrange(
            "p (c e) -> p c e", c=NSC).bitcast(I32) for i in range(2))
        int_lo = acc[:, 0:NSC * P].rearrange("p (c e) -> p c e", c=NSC).bitcast(I32)
        int_hi = acc[:, NSC * P:2 * NSC * P].rearrange("p (c e) -> p c e", c=NSC).bitcast(I32)
        f_src, f_dst = (part[:, 0:2 * NSC * P].bitcast(F32).rearrange("p (c e) -> p c e", c=NSC) for part in qparts[0:2])
        f_lo = tmp[:, :, :].rearrange("p a b -> p (a b)")[:, 0:NSC * P].rearrange("p (c e) -> p c e", c=NSC)
        f_hi = tmp[:, :, :].rearrange("p a b -> p (a b)")[:, NSC * P:2 * NSC * P].rearrange("p (c e) -> p c e", c=NSC)
        f_pen = acc[:, 2 * NSC * P:3 * NSC * P].rearrange("p (c e) -> p c e", c=NSC)

        def load_blocks(engine, s):
            return nc.values_load_multi_w_load_instructions(
                wrow[0:1, bass.ds(s, GROUP)], engines=[engine], min_val=0, max_val=(NB - 1) * PITCH,
                skip_runtime_bounds_check_because="the setup writes at most (NB - 1) * PITCH")[1]

        block = ctx.enter_context(nc.Block())

        @block.sync
        def _(sp):
            sp.dma_start(tmp[0:TILE_ROWS, 0:16 * P // D + 1, :].rearrange("p a b -> p (a b)")[:, 0:16 * P].bitcast(I32),
                         ins["dst"].rearrange("(p t) -> p t", p=TILE_ROWS)).then_inc(s_load_dst, 16)
            xv = ins["x"][0:(NB - 1) * P, :].rearrange("(w p) c -> p w c", p=P)
            sp.wait_ge(s_const, 1)
            sp.dma_start(xres[:, 0:NB - 1, :], xv).then_inc(s_load, 16)
            sp.dma_start(xres[0:TAIL, NB - 1, :], ins["x"][(NB - 1) * P:, :]).then_inc(s_load, 16)
            for t, n in ((w0, "L0_gnn_W"), (w1, "L1_gnn_weight"), (w3a, "L3_gnn_W1"), (w3b, "L3_gnn_W2"), (we, "L2_gnn_We")):
                sp.dma_start(t[0:D, 0:D], ins[n]).then_inc(s_load, 16)
            for i, n in enumerate("qkv"):
                sp.dma_start(wqkv[0:D, i * D:(i + 1) * D], ins[f"L2_gnn_W{n}"]).then_inc(s_load, 16)
                sp.dma_start(wqkv[D:D + 1, i * D:(i + 1) * D], ins[f"L2_gnn_b{n}"].rearrange("(a c) -> a c", a=1)).then_inc(s_load, 16)
            for t, n in ((w1, "L1_gnn_bias"), (we, "L2_gnn_be")):
                sp.dma_start(t[D:D + 1, :], ins[n].rearrange("(a c) -> a c", a=1)).then_inc(s_load, 16)
            for n in VECTORS:
                v = ins[n]
                v = v.rearrange("h c -> (h c)") if len(v.shape) == 2 else v
                sp.dma_start(vrow[n], v.partition_broadcast(P)).then_inc(s_load, 16)

            sp.wait_ge(s_eidx, 1)
            for i in range(2):
                sp.dma_start(row_dram[i, :].rearrange("(c p) -> p c", p=P), rows_cols[i],
                             allow_slow_non_contiguous=True).then_inc(s_rows[i], 16)
            for i, r in enumerate((wrow, erow)):
                sp.wait_ge(s_rows[i], 16)
                sp.dma_start(r[:, 0:STEPS], row_dram[i:i + 1, 0:STEPS]).then_inc(s_wrap, 16)
                sp.dma_start(r[:, STEPS:], row_dram[i:i + 1, 0:BODY]).then_inc(s_wrap, 16)

            def store_table(i, view):
                sp.wait_ge(s_ready, READY[f"table{i}"])
                sp.dma_start(table[i].rearrange("(w p) c -> p w c", p=P), view).then_inc(s_table, 16)

            attr = ins["edge_attr_96"].rearrange("(t p) c -> p t c", p=P)
            proj = eproj.rearrange("(t p) c -> p t c", p=P)

            def load_attributes(q, first, n):
                sp.dma_start(eattr[:, q * GROUP:q * GROUP + n, :], attr[:, bass.ds(first, n), :]).then_inc(ein[q], 16)

            def store_projected(q, i, first, n):
                sp.wait_ge(eout_ready[q], i)
                sp.dma_start(proj[:, bass.ds(first, n), :], eout[:, q, 0:n, :]).then_inc(estored[q], 16)

            for q in range(GROUPS):
                sp.sem_inc(estored[q], 16)
            store_table(0, tab100)
            for q in range(GROUPS):
                load_attributes(q, q * E0, E0)
            with sp.Fori(1, ITERS, 1) as i:
                for q in range(GROUPS):
                    sp.wait_ge(eturned[q], i)
                    load_attributes(q, (i * GROUPS + q) * E0, E0)
                    store_projected(q, i, (i * GROUPS - GROUPS + q) * E0, E0)
            base = ITERS * GROUPS * E0
            for q in range(GROUPS):
                sp.wait_ge(eturned[q], ITERS)
                load_attributes(q, base + q * E1, E1)
                store_projected(q, ITERS, base - (GROUPS - q) * E0, E0)
            store_table(1, tab96)
            with sp.Fori(1, ITERS, 1) as k:
                i = sp.snap(k + ITERS)
                for q in range(GROUPS):
                    sp.wait_ge(eturned[q], i)
                    load_attributes(q, (k * GROUPS + q) * E1 + base, E1)
                    store_projected(q, i, (k * GROUPS - GROUPS + q) * E1 + base, E1)
            for q in range(GROUPS):
                store_projected(q, 2 * ITERS, base + (ITERS * GROUPS - GROUPS + q) * E1, E1)
            for q in range(GROUPS):
                sp.wait_ge(estored[q], 2 * ITERS * 16 + 16)
            store_table(2, tab192)
            sp.wait_ge(s_wrap, 64)

            def load_projected(s, q):
                at = nc.values_load_multi_w_load_instructions(
                    erow[0:1, bass.ds(s + q * GROUP, GROUP)], engines=[mybir.EngineType.SP], min_val=0,
                    max_val=(REACHED - 1) * P, skip_runtime_bounds_check_because="the setup writes at most (REACHED - 1) * P")[1]
                for j in range(GROUP):
                    sp.dma_start(eattr[:, q * GROUP + j, :], eproj[bass.ds(at[j], P), :]).then_inc(
                        eloaded[q], 16)

            for q in range(GROUPS):
                load_projected(0, q)
            with sp.Fori(1, ITERS, 1) as k:
                for q in range(GROUPS):
                    sp.wait_ge(link[q][1], k + ITERS)
                    load_projected(k * BODY, q)
            store_table(3, tab96)
            store_table(4, tab96)
            for h, (a, b) in enumerate(HALVES):
                sp.wait_ge(s_ready, READY[f"out{h}"])
                z = min(b, NB - 1)
                sp.dma_start(out[a * P:z * P, :].rearrange("(w p) c -> p w c", p=P), xres[:, a:z, :]).then_inc(s_out, 16)
            sp.dma_start(out[(NB - 1) * P:, :], xres[0:TAIL, NB - 1, :]).then_inc(s_out, 16)
            sp.wait_ge(s_table, 16 * 5)
            sp.wait_ge(s_out, 48)

        @block.gpsimd
        def _(pool):
            g = nc.gpsimd
            g.memset(xres[:, NB - 1, :], 0.0).then_inc(s_const, 1)
            g.memset(ones[:, :], 1.0).then_inc(s_const, 1)
            g.memset(zero_bf[:, :], 0.0).then_inc(s_const, 1)
            g.memset(eps[:, :], 1e-5).then_inc(s_const, 1)
            g.iota(iota[:, :], [[1, P]], base=0, channel_multiplier=0, allow_small_or_imprecise_dtypes=True).then_inc(s_const, 1)
            g.iota(iota_hi[:, :], [[1, NB]], base=0, channel_multiplier=0, allow_small_or_imprecise_dtypes=True).then_inc(s_const, 1)
            g.iota(step_col, [[P, NSC]], base=0, channel_multiplier=1, allow_small_or_imprecise_dtypes=True).then_inc(s_const, 1)
            g.iota(block_end, [[P, NB]], base=P, channel_multiplier=0, allow_small_or_imprecise_dtypes=True).then_inc(s_const, 1)
            pool.wait_ge(s_const, 8)
            g.affine_select(out=ident[:, :], in_=ones[:, :], compare_op=ALU.is_equal, fill=0.0, base=0,
                            pattern=[[-1, P]], channel_multiplier=1).then_inc(s_const, 1)
            pool.wait_ge(s_const, 9)
            g.tensor_copy(ident_bf[:, :], ident[:, :]).then_inc(s_const, 1)
            pool.wait_ge(s_eidx, 1)
            for c in range(NSC):
                for arr, n in ((steps_src, "src"), (steps_dst, "dst")):
                    pool.indirect_dma_start(arr[:, c, :], None, ins[n].rearrange("(t e) -> t e", e=P),
                                            bass.IndirectOffsetOnAxis(ap=tile_idx[:, c:c + 1], axis=0)).then_inc(s_steps, 16)
            pool.wait_ge(s_ready, READY["gmax"])
            g.partition_all_reduce(gmax[:, 1, :], gmax[:, 0, :], P, RMAX).then_inc(s_gmax, 1)

            def gather_pass(number, width):
                pool.wait_ge(s_table, 16 * (number + 1))
                with pool.Fori(number * ITERS, (number + 1) * ITERS, 1) as i:
                    for q in range(GROUPS):
                        pool.wait_ge(idx_ready[q], i + 1)
                        pool.sem_inc(pool_step, 1)
                        for j in range(GROUP):
                            slot = q * GROUP + j
                            pool.indirect_dma_start(
                                gath[:, slot, 0:width], None, table[number],
                                bass.IndirectOffsetOnAxis(ap=cols[:, q, j, 0:1], axis=0)).then_inc(gathered[q], 16)

            for number, width in enumerate([T0, D, 2 * D, D, D]):
                if number == 2:
                    pool.wait_ge(s_ready, READY["project1"])
                    g.memset(acc[:, :], 0.0).then_inc(s_clear, 1)
                gather_pass(number, width)

        @block.tensor
        def _(pe):
            mm = nc.tensor.matmul
            pe.wait_ge(s_const, 10)
            pe.wait_ge(s_setup_dve, 1)
            mm(ps[:, 0, 0:NB], ones[0:TILE_ROWS, :], tile_last[0:TILE_ROWS, :], start=True, stop=True).then_inc(s_setup_pe, 1)

            def project(call, weights, width, k=D):
                with pe.Fori(call * PROJ_ITERS, (call + 1) * PROJ_ITERS, 1) as i:
                    pe.wait_ge(proj_staged, i + 1)
                    for half, blocks in enumerate((range(0, 4), range(4, PB))):
                        pe.wait_ge(proj_sb[half], i + 1)
                        for b in blocks:
                            t = nc.tensor.transpose(ps[0:D, half, b % 4 * P:b % 4 * P + P],
                                                    staged[:, b, :], ident[:, :])
                        t.then_inc(proj_turned[half], 1)
                    for b in range(PB):
                        if b % 4 == 0:
                            pe.wait_ge(proj_sb[b // 4], i + 2)
                        pe.wait_ge(proj_out[b], i + 1)
                        if b == 0:
                            pe.wait_ge(proj_out[PB - 1], i + 1)
                        if b == PB - 1:
                            pe.wait_ge(proj_out[0], i + 2)
                        mm(ps[:, 2 + b % 6, 0:width], xt[0:k, b, :], weights[0:k, 0:width],
                           start=True, stop=True).then_inc(proj_done[b], 1)

            project(0, w0, D + 2 * H0)
            pe.wait_ge(s_setup_dve, 2)
            for k, arr in enumerate((f_src, f_dst, f_lo, f_hi)):
                for c in range(NSC):
                    n = k * NSC + c
                    if n >= 8:
                        pe.wait_ge(s_setup_dve, 2 + n - 7)
                    nc.tensor.transpose(ps[:, n % 8, 0:P], arr[:, c, :],
                                        ident[:, :]).then_inc(s_setup_pe, 1)

            def block_regs(s):
                return load_blocks(mybir.EngineType.PE, s)

            def turn(q, i, j):
                pe.wait_ge(onehot_ready[q], i + 1)
                for t in range(GROUP):
                    m = nc.tensor.transpose(ps[:, 0, :].bitcast(BF16)[:, t * P:t * P + P], onehot[:, q, t, :], ident_bf[:, :])
                m.then_inc(turned[q], 1)

            def spread_parts(q, j, s):
                w = block_regs(s)
                pe.wait_ge(turned_sb[q], j + 1)
                for t in range(GROUP):
                    m = mm(ps[:, 1 + q % 2, t * PARTS0:(t + 1) * PARTS0], onehot_t[:, t, :],
                           qparts[0][:, bass.ds(w[t], PARTS0)], start=True, stop=True)
                m.then_inc(spread[q], 1)

            def spread_rows(q, j, s):
                bank, width = 2 + q % 2, D
                w = block_regs(s)
                pe.wait_ge(turned_sb[q], j + 1)
                for t in range(GROUP):
                    for n, part in enumerate(qparts):
                        m = mm(ps[:, bank, t * width:(t + 1) * width], onehot_t[:, t, :], part[:, bass.ds(w[t], width)],
                               start=(n == 0), stop=(n == len(qparts) - 1))
                m.then_inc(spread[q], 1)

            def sums(q, i, width, source):
                pe.wait_ge(onehot_f_ready[q], i + 1)
                for t in range(GROUP):
                    m = mm(ps[:, 6 + q % 2, t * PITCH:t * PITCH + width], onehot_f[:, q, t, :], source(t),
                           start=True, stop=True)
                m.then_inc(summed[q], 1)

            def turn_attributes(q, i, n):
                pe.wait_ge(ein[q], i * 16 + 16)
                for t in range(n):
                    m = nc.tensor.transpose(ps[0:D, 4, t * P:t * P + P], eattr[:, q * GROUP + t, :], ident[:, :])
                m.then_inc(eturned[q], 1)

            def project_attributes(q, i, n):
                pe.wait_ge(eturned_sb[q], i + 1)
                for t in range(n):
                    m = mm(ps[:, 5, t * D:(t + 1) * D], eattr_t[:, t, :], we[:, :], start=True, stop=True)
                m.then_inc(eprojected[q], 1)

            pe.wait_ge(s_wrap, 64)
            pe.wait_ge(s_ready, READY["pass0"])
            mm(ps[:, 3, 0:NB], zero_bf[:, :], zero_bf[:, 0:NB], start=True, stop=False, skip_group_check=True)

            def count_sources(q, i):
                pe.wait_ge(histo[q], i + 1)
                for t in range(GROUP):
                    mm(ps[:, 3, 0:NB], src_lo[:, q % 2, t, :], src_hi[:, q % 2, t, :], start=False, stop=False,
                       skip_group_check=True)

            def slot0(q, i, last=False):
                b, ib = (q + 1, i) if q < 3 else (0, i + 1)
                c, ic = (q + 2, i) if q < 2 else (q - 2, i + 1)
                if not (last and q >= 2):
                    turn(c, ic, ic)
                count_sources(q, i)
                pe.wait_ge(msgs[q], i + 1)
                sums(q, i, D + H0 + 1, lambda t: msg[:, q, t, 0:D + H0 + 1])
                if not (last and q >= 2):
                    spread_parts(c, ic, ic * BODY + c * GROUP)
                project_attributes(q, i, E0)
                if not (last and q == 3):
                    turn_attributes(b, ib, E0)

            for q in (0, 1):
                turn(q, 0, 0)
                spread_parts(q, 0, q * GROUP)
            turn_attributes(0, 0, E0)
            with pe.Fori(0, ITERS - 1, 1) as i:
                for q in range(GROUPS):
                    slot0(q, i)
            for q in range(GROUPS):
                slot0(q, ITERS - 1, last=True)
            mm(ps[:, 3, 0:NB], zero_bf[:, :], zero_bf[:, 0:NB], start=False, stop=True,
               skip_group_check=True).then_inc(s_setup_pe, 1)

            def linear_pass(number, n):
                with pe.Fori(number * ITERS, (number + 1) * ITERS, 1) as i:
                    g = pe.snap((i + 1) * (16 * GROUP))
                    for q in range(GROUPS):
                        if n:
                            turn_attributes(q, i, n)
                        pe.wait_ge(onehot_f_ready[q], i + 1)
                        pe.wait_ge(added[(q + 2) % GROUPS], i + 1)
                        pe.wait_ge(gathered[q], g)
                        for t in range(GROUP):
                            m = mm(ps[:, 6 + q % 2, t * PITCH:t * PITCH + D], onehot_f[:, q, t, :],
                                   gath[:, q * GROUP + t, 0:D], start=True, stop=True)
                        m.then_inc(summed[q], 1)
                        if n:
                            project_attributes(q, i, n)

            linear_pass(1, E1)
            project(1, w1, D, D + 1)

            project(2, wqkv, 3 * D, D + 1)
            pe.wait_ge(s_ready, READY["pass2"])

            def slot2(q, i, j, now, last=False):
                n = 1 if q >= 2 else 0
                c = (q + 2) % GROUPS
                if not (last and q >= 2):
                    turn(c, i + n, j + n)
                pe.wait_ge(msgs[q], j + 1)
                sums(q, i, D + H2, lambda t: msg[:, q, t, 0:D + H2])
                if not (last and q >= 2):
                    spread_rows(c, j + n, now + n * BODY + c * GROUP)

            for q in (0, 1):
                turn(q, 2 * ITERS, ITERS)
                spread_rows(q, ITERS, q * GROUP)
            with pe.Fori(2 * ITERS, 3 * ITERS - 1, 1) as i:
                j = pe.snap(i - ITERS)
                now = pe.snap((i - 2 * ITERS) * BODY)
                for q in range(GROUPS):
                    slot2(q, i, j, now)
            for q in range(GROUPS):
                slot2(q, 3 * ITERS - 1, 2 * ITERS - 1, (ITERS - 1) * BODY, last=True)
            project(3, w3a, D)
            linear_pass(3, 0)
            project(4, w3b, D)
            linear_pass(4, 0)

        @block.scalar
        def _(act):
            for s in proj_sb:
                act.sem_inc(s, 1)
            act.wait_ge(s_const, 10)

            def project(call):
                act.wait_ge(s_ready, READY[f"project{call}"])
                source = (xres, tmp, xres, xres, tmp)[call][:, :, :].rearrange("p w c -> p (w c)")
                with act.Fori(call * PROJ_ITERS, (call + 1) * PROJ_ITERS, 1) as i:
                    nc.scalar.activation(staged[:, :, :].rearrange("p b c -> p (b c)"),
                                         source[:, bass.ds((i - call * PROJ_ITERS) * PB * D, PB * D)],
                                         ACT.Relu if call == 4 else ACT.Copy).then_inc(proj_staged, 1)
                    for half, (a, b) in enumerate(((0, 4), (4, PB))):
                        act.wait_ge(proj_turned[half], i + 1)
                        nc.scalar.activation(xt[0:D, a:b, :], ps[0:D, half, 0:(b - a) * P].rearrange("p (b c) -> p b c", c=P),
                                             ACT.Copy).then_inc(proj_sb[half], 1)

            def whole(need, out_, in_, func, **kw):
                act.wait_ge(s_ready, READY[need])
                nc.scalar.activation(out_, in_, func, **kw).then_inc(s_act, 1)

            def norm_roots(name):
                for h, (a, b) in enumerate(HALVES):
                    whole(f"{name}_sq{h}", tab96[:, a:b, :], tmp[:, a:b, :], ACT.Square)
                whole(f"{name}_var", std, var, ACT.Sqrt, bias=eps[:, 0:1], scale=1.0 / D)

            def copy_turned(q, j):
                act.wait_ge(turned[q], j + 1)
                nc.scalar.activation(onehot_t[:, :, :], ps[:, 0, :].bitcast(BF16)[:, 0:GROUP * P].rearrange(
                    "p (j e) -> p j e", j=GROUP), ACT.Copy).then_inc(turned_sb[q], 1)

            def widen(q, i):
                act.wait_ge(onehot_ready[q], i + 1)
                nc.scalar.activation(onehot_f[:, q, :, :], onehot[:, q, :, :], ACT.Copy).then_inc(onehot_f_ready[q], 1)

            def exp_logits(q, j, heads_):
                act.wait_ge(logits[q], j + 1)
                nc.scalar.activation(msg[:, q, :, D:D + heads_], logit[:, q % 2, :, 0:heads_], ACT.Exp).then_inc(exps[q], 1)

            def copy_attributes(q, i, n):
                act.wait_ge(eturned[q], i + 1)
                nc.scalar.activation(eattr_t[0:D, 0:n, :], ps[0:D, 4, 0:n * P].rearrange("p (j e) -> p j e", j=n),
                                     ACT.Copy).then_inc(eturned_sb[q], 1)

            def copy_projected(q, i, n):
                act.wait_ge(eprojected[q], i + 1)
                act.wait_ge(estored[q], i * 16 + 16)
                nc.scalar.activation(eout[:, q, 0:n, :], ps[:, 5, 0:n * D].rearrange("p (j c) -> p j c", j=n),
                                     ACT.Copy).then_inc(eout_ready[q], 1)

            project(0)
            whole("self", accv[:, :, D:D + H0], accv[:, :, D:D + H0], ACT.Exp)

            def slot0(q, i, last=False):
                b, ib = (q + 1, i) if q < 3 else (0, i + 1)
                c, ic = (q + 2, i) if q < 2 else (q - 2, i + 1)
                if not (last and q >= 2):
                    copy_turned(c, ic)
                if not (last and q == 3):
                    exp_logits(b, ib, H0)
                if not (last and q >= 2):
                    widen(c, ic)
                copy_projected(q, i, E0)
                if not (last and q == 3):
                    copy_attributes(b, ib, E0)

            for q in (0, 1):
                copy_turned(q, 0)
            for q in (0, 1):
                widen(q, 0)
            exp_logits(0, 0, H0)
            copy_attributes(0, 0, E0)
            with act.Fori(0, ITERS - 1, 1) as i:
                for q in range(GROUPS):
                    slot0(q, i)
            for q in range(GROUPS):
                slot0(q, ITERS - 1, last=True)
            norm_roots("n0")
            norm_roots("n1")
            whole("roots", node[:, 6:9, :], node[:, 6:9, :], ACT.Sqrt)
            with act.Fori(ITERS, 2 * ITERS, 1) as i:
                for q in range(GROUPS):
                    widen(q, i)
                    if q:
                        copy_projected(q - 1, i, E1)
                    copy_attributes(q, i, E1)
                copy_projected(GROUPS - 1, i, E1)
            project(1)
            norm_roots("n2")
            project(2)

            def slot2(q, i, j, last=False):
                n = 1 if q >= 2 else 0
                c = (q + 2) % GROUPS
                if not (last and q >= 2):
                    copy_turned(c, j + n)
                if not (last and q == 3):
                    exp_logits((q + 1) % GROUPS, j + (1 if q == 3 else 0), H2)
                if not (last and q >= 2):
                    widen(c, i + n)

            for q in (0, 1):
                copy_turned(q, ITERS)
            for q in (0, 1):
                widen(q, 2 * ITERS)
            exp_logits(0, ITERS, H2)
            with act.Fori(ITERS, 2 * ITERS - 1, 1) as j:
                i = act.snap(j + ITERS)
                for q in range(GROUPS):
                    slot2(q, i, j)
            for q in range(GROUPS):
                slot2(q, 3 * ITERS - 1, 2 * ITERS - 1, last=True)
            norm_roots("n3")
            for number in (3, 4):
                project(number)
                whole(f"table{number}", accv[:, :, 0:D], tab96, ACT.Copy)
                with act.Fori(number * ITERS, (number + 1) * ITERS, 1) as i:
                    for q in range(GROUPS):
                        widen(q, i)
            norm_roots("n4")

        @block.vector
        def _(dve):
            v = nc.vector
            links = [0]
            told = [0]

            def chain(ins):
                links[0] += 1
                ins.then_inc(chain_dve, 1)
                dve.wait_ge(chain_dve, links[0])

            def ready(name):
                told[0] += 1
                assert READY[name] == told[0], name
                dve.sem_inc(s_ready, 1)

            def await_act(name):
                dve.wait_ge(s_act, ACT_DONE[name])

            def copy_columns(q, s):
                v.tensor_copy(cols[:, q, :, :], steps[:, bass.ds(s, GROUP), :]).then_inc(idx_ready[q], 1)

            def make_onehot(q, t):
                o = v.tensor_scalar(onehot[:, q, t, :], iota[:, :], dcol[:, q, t:t + 1], None, ALU.is_equal)
                if t == GROUP - 1:
                    o.then_inc(onehot_ready[q], 1)

            def turn_over(q, i, s, nxt):
                w = load_blocks(mybir.EngineType.DVE, s)
                dve.wait_ge(summed[q], i + 1)
                copy_columns(q, nxt)
                return w

            def add(q, t, i, w, width):
                if t:
                    dve.wait_ge(add_link[q * GROUP + t], i + 1)
                elif q:
                    dve.wait_ge(added[q - 1], i + (1 if q - 1 < 2 else 2))
                else:
                    dve.wait_ge(added[GROUPS - 1], i + 1)
                a = v.tensor_tensor(acc[:, bass.ds(w[t], width)], acc[:, bass.ds(w[t], width)],
                                    ps[:, 6 + q % 2, t * PITCH:t * PITCH + width], ALU.add)
                a.then_inc(added[q] if t == GROUP - 1 else add_link[q * GROUP + t + 1], 1)

            def add_and_refill(q, i, s, nxt, width):
                w = turn_over(q, i, s, nxt)
                for t in range(GROUP):
                    add(q, t, i, w, width)
                    if t == 0:
                        dve.wait_ge(idx_ready[q], i + 2)
                    make_onehot(q, t)

            def project(call, take):
                with dve.Fori(call * PROJ_ITERS, (call + 1) * PROJ_ITERS, 1) as i:
                    first = dve.snap(i * PB - call * NB)
                    for b in range(PB):
                        dve.wait_ge(proj_done[b], i + 1)
                        take(first + b, ps[:, 2 + b % 6, :]).then_inc(proj_out[b], 1)
                for b in range(PB):
                    dve.wait_ge(proj_out[b], (call + 1) * PROJ_ITERS + 1)

            def norm(name, src, dst, told_of=()):
                chain(v.tensor_reduce(mean, src, AX, ALU.add))
                chain(v.tensor_scalar(mean, mean, 1.0 / D, None, ALU.mult))
                for h, (a, b) in enumerate(HALVES):
                    chain(v.tensor_tensor(tmp[:, a:b, :], src[:, a:b, :], bc(mean[:, a:b], D), ALU.subtract))
                    ready(f"{name}_sq{h}")
                for h, (a, b) in enumerate(HALVES):
                    await_act(f"{name}_sq{h}")
                    chain(v.tensor_reduce(var[:, a:b], tab96[:, a:b, :], AX, ALU.add))
                ready(f"{name}_var")
                await_act(f"{name}_var")
                chain(v.reciprocal(rstd, std))
                for h, (a, b) in enumerate(HALVES if told_of else ((0, NB),)):
                    chain(v.tensor_tensor(dst[:, a:b, :], tmp[:, a:b, :], bc(rstd[:, a:b], D), ALU.mult))
                    if told_of:
                        ready(told_of[h])

            def split(x, parts):
                for n, part in enumerate(parts):
                    chain(v.tensor_copy(part, x))
                    if n < 2:
                        chain(v.tensor_tensor(x, x, part, ALU.subtract))

            xres_flat = xres[:, :, :].rearrange("p w c -> p (w c)")
            tmp_flat = tmp[:, :, :].rearrange("p w c -> p (w c)")

            def ones_row():
                chain(v.memset(xt[D:D + 1, :, :], 1.0))

            for s in (added[2], added[3], *proj_out):
                dve.sem_inc(s, 1)
            dve.wait_ge(s_const, 10)
            dve.wait_ge(s_load_dst, 16)
            R = TILE_ROWS
            edge_dst = tmp[0:R, :, :].rearrange("p a b -> p (a b)")[:, 0:16 * P].bitcast(I32)
            chain(v.tensor_reduce(lmax[0:R, :], edge_dst.rearrange("p (t e) -> p t e", e=P), AX, ALU.max))
            over = cmp[0:R, 0:NB * 16].rearrange("p (w t) -> p w t", w=NB)
            chain(v.tensor_tensor(over, mid(lmax[0:R, :], NB), bc(block_end[0:R, :], 16), ALU.is_lt))
            chain(v.tensor_reduce(tile_last[0:R, :], over, AX, ALU.add))
            dve.sem_inc(s_setup_dve, 1)
            dve.wait_ge(s_setup_pe, 1)
            chain(v.tensor_tensor(advance, ps[:, 0, 0:NB], iota_hi[:, :], ALU.add))
            past = cmp[:, 0:NSC * (NB - 1)].rearrange("p (c w) -> p c w", c=NSC)
            chain(v.tensor_tensor(past, mid(advance[:, 0:NB - 1], NSC), bc(step_col, NB - 1), ALU.is_lt))
            chain(v.tensor_reduce(wcol, past, AX, ALU.add))
            chain(v.tensor_tensor(ecol, step_col, wcol, ALU.subtract))
            chain(v.tensor_scalar(ecol, ecol, float(REACHED - 1), None, ALU.min))
            chain(v.tensor_copy(tile_idx, ecol))
            chain(v.tensor_scalar(rows_cols[0], wcol, float(PITCH), None, ALU.mult))
            chain(v.tensor_scalar(rows_cols[1], ecol, float(P), None, ALU.mult))
            chain(v.tensor_scalar(w128, wcol, float(P), None, ALU.mult))
            dve.sem_inc(s_eidx, 1)

            dve.wait_ge(s_load, 16 * LOADS)
            for at_, att in ((D, "L0_gnn_att_src"), (T0, "L0_gnn_att_dst")):
                chain(v.tensor_tensor(eattr[0:D, 0, :], w0[:, 0:D], vrow[att][0:D, :], ALU.mult))
                chain(v.tensor_reduce(w0[:, at_:at_ + H0], eattr[0:D, 0, :].rearrange("p (h c) -> p h c", h=H0), AX, ALU.add))
            ready("project0")
            there_flat = there[:, :, :].rearrange("p w c -> p (w c)")

            def take0(b, p):
                v.tensor_copy(tab[:, bass.ds(b * T0, T0)], p[:, 0:T0])
                return v.tensor_copy(there_flat[:, bass.ds(b * (2 * H0), H0)], p[:, T0:T0 + H0])

            project(0, take0)
            a_src, a_dst, guard = tab100[:, :, D:T0], there[:, :, 0:H0], there[:, :, H0:]
            chain(v.tensor_reduce(gmax[:, 0, :], a_src.rearrange("p w h -> p h w"), AX, ALU.max))
            ready("table0")
            ready("gmax")

            dve.wait_ge(s_steps, 16 * 2 * NSC)
            chain(v.tensor_copy(f_src, steps_src))
            chain(v.tensor_copy(f_dst, steps_dst))
            chain(v.tensor_tensor(f_dst, f_dst, bc(w128, P), ALU.subtract))
            chain(v.tensor_scalar(int_lo, steps_src, P - 1, None, ALU.bitwise_and))
            chain(v.tensor_scalar(int_hi, steps_src, P.bit_length() - 1, None, ALU.logical_shift_right))
            chain(v.tensor_copy(f_lo, int_lo))
            chain(v.tensor_copy(f_hi, int_hi))
            chain(v.tensor_scalar(f_pen, f_dst, 0.0, BIG, ALU.is_lt, ALU.mult))
            chain(v.tensor_tensor(f_hi, f_hi, f_pen, ALU.add))
            chain(v.tensor_scalar(f_pen, f_dst, float(P), BIG, ALU.is_ge, ALU.mult))
            chain(v.tensor_tensor(f_hi, f_hi, f_pen, ALU.add))
            dve.sem_inc(s_setup_dve, 1)
            chain(v.memset(steps[:, :, :].bitcast(BF16)[:, :, 5], 0.0))
            for k, dst in enumerate((src_s, drel_s, lo_s, hi_s)):
                for c in range(NSC):
                    n = k * NSC + c
                    m = min(P, STEPS - c * P)
                    dve.wait_ge(s_setup_pe, 2 + n)
                    v.tensor_copy(dst[:, c * P:c * P + m], ps[:, n % 8, 0:m]).then_inc(s_setup_dve, 1)
            dve.wait_ge(s_setup_dve, 2 + 4 * NSC)
            chain(v.tensor_copy(steps[:, STEPS:, :], steps[:, 0:BODY, :]))
            chain(v.memset(eattr_t[D:D + 1, :, :], 1.0))
            chain(v.memset(msg[:, :, :, D + H0:D + H0 + 1], 1.0))
            for q in range(GROUPS):
                copy_columns(q, q * GROUP)
                dve.wait_ge(idx_ready[q], 1)
                for t in range(GROUP):
                    make_onehot(q, t)
            dve.wait_ge(s_wrap, 64)

            htab = tab100[:, :, 0:D]
            by_head = tmp[:, :, :].rearrange("p w (h c) -> p w h c", h=H0)
            hv = heads[:, 0, 0:NB * H0].rearrange("p (w h) -> p w h", w=NB)
            ex_self = accv[:, :, D:D + H0]
            dve.wait_ge(s_gmax, 1)
            chain(v.tensor_tensor(hv, a_dst, mid(gmax[:, 1, :], NB), ALU.add))
            chain(v.scalar_tensor_tensor(out=guard, in0=hv, scalar=0.2, in1=hv, op0=ALU.mult, op1=ALU.max))
            chain(v.tensor_tensor(hv, a_src, a_dst, ALU.add))
            chain(v.scalar_tensor_tensor(out=hv, in0=hv, scalar=0.2, in1=hv, op0=ALU.mult, op1=ALU.max))
            chain(v.tensor_tensor(hv, hv, guard, ALU.subtract))
            chain(v.tensor_scalar(ex_self, hv, 0.0, None, ALU.min))
            ready("self")
            await_act("self")
            chain(v.tensor_tensor(accv[:, :, 0:D].rearrange("p w (h c) -> p w h c", h=H0),
                                  htab.rearrange("p w (h c) -> p w h c", h=H0), bc(ex_self, C0), ALU.mult))
            chain(v.memset(accv[:, :, D + H0:D + H0 + 1], 0.0))
            split(there[:, :, :], [qpart_v[0][:, :, n * 2 * H0:(n + 1) * 2 * H0] for n in range(3)])
            ready("pass0")

            def messages(q, j, h, c, at):
                dve.wait_ge(exps[q], j + 1)
                v.tensor_tensor(msg[:, q, :, 0:D].rearrange("p j (h c) -> p j h c", h=h),
                                gath[:, q * GROUP:(q + 1) * GROUP, at:at + D].rearrange("p j (h c) -> p j h c", h=h),
                                bc(msg[:, q, :, D:D + h], c), ALU.mult).then_inc(msgs[q], 1)

            def body0(i, first):
                g = (i + 1) * (16 * GROUP) if first else dve.snap((i + 1) * (16 * GROUP))
                now = i * BODY if first else dve.snap(i * BODY)
                prev = None if first else dve.snap(i - 1)
                for q in range(GROUPS):
                    p = (q + 2) % GROUPS
                    pi, ps_, pn = (i, now, now + BODY) if q >= 2 else (prev, now - BODY if not first else None, now)
                    old = q >= 2 or not first
                    width = D + H0 + 1
                    if old:
                        w = turn_over(p, pi, ps_ + p * GROUP, pn + p * GROUP)
                    dve.wait_ge(gathered[q], g)
                    dve.wait_ge(spread[q], i + 1)
                    parts = ps[:, 1 + q % 2, 0:GROUP * PARTS0].rearrange("p (j k c) -> p j c k", j=GROUP, k=3)
                    dst = dvals[:, q % 2, :, :]
                    v.tensor_reduce(dst, parts, AX, ALU.add).then_inc(link[q][3], 1)
                    if old:
                        dve.wait_ge(idx_ready[p], pi + 2)
                        make_onehot(p, 0)
                    dve.wait_ge(link[q][3], i + 1)
                    lg = logit[:, q % 2, :, 0:H0]
                    v.tensor_tensor(lg, gath[:, q * GROUP:(q + 1) * GROUP, D:D + H0], dst[:, :, 0:H0], ALU.add).then_inc(link[q][0], 1)
                    if old:
                        add(p, 0, pi, w, width)
                    dve.wait_ge(link[q][0], i + 1)
                    v.scalar_tensor_tensor(out=lg, in0=lg, scalar=0.2, in1=lg, op0=ALU.mult, op1=ALU.max).then_inc(link[q][1], 1)
                    if old:
                        make_onehot(p, 1)
                    dve.wait_ge(link[q][1], i + 1)
                    v.tensor_tensor(lg, lg, dst[:, :, H0:2 * H0], ALU.subtract).then_inc(link[q][2], 1)
                    if old:
                        add(p, 1, pi, w, width)
                    dve.wait_ge(link[q][2], i + 1)
                    v.tensor_scalar(lg, lg, 0.0, None, ALU.min).then_inc(logits[q], 1)
                    for t in range(GROUP):
                        v.tensor_scalar(src_lo[:, q % 2, t, :], iota[:, :], locol[:, q, t:t + 1], None, ALU.is_equal)
                        if old and t % 2 == 0:
                            make_onehot(p, 2 + t // 2)
                            add(p, 2 + t // 2, pi, w, width)
                    v.tensor_tensor(src_hi[:, q % 2, :, :], mid(iota_hi[:, :], GROUP),
                                    bc(hicol[:, q, :], NB), ALU.is_equal).then_inc(histo[q], 1)
                    messages(q, i, H0, C0, 0)

            def last_groups(i, now, width):
                for q in (2, 3):
                    add_and_refill(q, i, now + q * GROUP, now + BODY + q * GROUP, width)

            body0(0, True)
            with dve.Fori(1, ITERS, 1) as i:
                body0(i, False)
            last_groups(ITERS - 1, (ITERS - 1) * BODY, D + H0 + 1)

            def pass_done(number):
                dve.wait_ge(added[GROUPS - 1], (number + 1) * ITERS + 1)

            pass_done(0)
            chain(v.tensor_scalar(hv, ex_self, 1e-16, None, ALU.add))
            chain(v.reciprocal(hv, hv))
            chain(v.tensor_tensor(by_head, accv[:, :, 0:D].rearrange("p w (h c) -> p w h c", h=H0), bc(hv, C0), ALU.mult))
            chain(v.tensor_tensor(tmp[:, :, :], tmp[:, :, :], mid(vrow["L0_gnn_bias"], NB), ALU.add))
            chain(v.tensor_tensor(tmp[:, :, :], tmp[:, :, :], xres[:, :, :], ALU.add))
            norm("n0", tmp[:, :, :], tmp[:, :, :])
            chain(v.tensor_tensor(tmp[:, :, :], tmp[:, :, :], mid(vrow["L0_gnn_gamma"], NB), ALU.mult))
            chain(v.tensor_tensor(tmp[:, :, :], tmp[:, :, :], mid(vrow["L0_gnn_beta"], NB), ALU.add))
            chain(v.scalar_tensor_tensor(out=xres[:, :, :], in0=tmp[:, :, :], scalar=0.0, in1=xres[:, :, :], op0=ALU.max, op1=ALU.add))
            norm("n1", xres[:, :, :], xres[:, :, :])
            dve.wait_ge(s_setup_pe, 2 + 4 * NSC)
            chain(v.tensor_copy(in_deg, accv[:, :, D + H0]))
            chain(v.tensor_copy(out_deg, ps[:, 3, 0:NB]))
            chain(v.tensor_scalar(ci, out_deg, 1.0, None, ALU.max))
            chain(v.tensor_scalar(cj, in_deg, 1.0, None, ALU.max))
            chain(v.tensor_scalar(dinv, in_deg, 1.0, None, ALU.add))
            chain(v.tensor_scalar(lone, in_deg, 0.0, None, ALU.is_equal))
            ready("roots")
            await_act("roots")
            chain(v.reciprocal(node[:, 6:9, :], node[:, 6:9, :]))

            def linear_pass(number):
                with dve.Fori(number * ITERS, (number + 1) * ITERS, 1) as i:
                    now = dve.snap((i - number * ITERS) * BODY)
                    nxt = dve.snap(now + BODY)
                    for q in range(GROUPS):
                        add_and_refill(q, i, now + q * GROUP, nxt + q * GROUP, D)
                pass_done(number)

            chain(v.tensor_tensor(tab96, xres[:, :, :], bc(ci, D), ALU.mult))
            ready("table1")
            chain(v.tensor_tensor(accv[:, :, 0:D], xres[:, :, :], bc(lone, D), ALU.mult))
            linear_pass(1)
            chain(v.tensor_tensor(tmp[:, :, :], accv[:, :, 0:D], bc(cj, D), ALU.mult))
            ones_row()
            ready("project1")
            project(1, lambda b, p: v.tensor_tensor(
                xres_flat[:, bass.ds(b * D, D)], xres_flat[:, bass.ds(b * D, D)], p[:, 0:D], ALU.add))
            norm("n2", xres[:, :, :], xres[:, :, :])

            ready("project2")
            for q in range(GROUPS):
                dve.wait_ge(estored[q], 2 * ITERS * 16 + 16)

            def take2(b, p):
                v.tensor_copy(tab[:, bass.ds(b * (2 * D), 2 * D)], p[:, D:3 * D])
                return v.tensor_scalar(tmp_flat[:, bass.ds(b * D, D)], p[:, 0:D], float(C2) ** -0.5, None, ALU.mult)

            project(2, take2)
            ready("table2")
            split(tmp[:, :, :], [part[:, :, 0:D] for part in qpart_v])
            dve.wait_ge(s_clear, 1)
            ready("pass2")

            def body2(i, first):
                keep = (lambda x: x) if first else dve.snap
                j = keep(i - ITERS)
                g = keep((i + 1) * (16 * GROUP))
                e = keep((i - 2 * ITERS + 1) * (16 * GROUP))
                now = keep((i - 2 * ITERS) * BODY)
                prev = None if first else dve.snap(i - 1)
                width = D + H2
                for q in range(GROUPS):
                    p = (q + 2) % GROUPS
                    pi, ps_, pn = (i, now, now + BODY) if q >= 2 else (prev, now - BODY if not first else None, now)
                    old = q >= 2 or not first
                    if old:
                        w = turn_over(p, pi, ps_ + p * GROUP, pn + p * GROUP)
                    dve.wait_ge(gathered[q], g)
                    dve.wait_ge(spread[q], j + 1)
                    at_dst = ps[:, 2 + q % 2, 0:GROUP * D].rearrange("p (j c) -> p j c", j=GROUP)
                    v.tensor_tensor(prod[:, :, :], gath[:, q * GROUP:(q + 1) * GROUP, 0:D], at_dst, ALU.mult).then_inc(link[q][0], 1)
                    if old:
                        add(p, 0, pi, w, width)
                    dve.wait_ge(eloaded[q], e)
                    dve.wait_ge(link[q][0], j + 1)
                    v.tensor_tensor(prod[:, :, :], prod[:, :, :], eattr[:, q * GROUP:(q + 1) * GROUP, :], ALU.mult).then_inc(link[q][1], 1)
                    if old:
                        add(p, 1, pi, w, width)
                    dve.wait_ge(link[q][1], j + 1)
                    lg = logit[:, q % 2, :, 0:H2]
                    v.tensor_reduce(lg, prod[:, :, :].rearrange("p j (h c) -> p j h c", h=H2), AX, ALU.add).then_inc(link[q][2], 1)
                    if old:
                        add(p, 2, pi, w, width)
                    dve.wait_ge(link[q][2], j + 1)
                    v.tensor_scalar(lg, lg, 5.0, -5.0, ALU.min, ALU.max).then_inc(logits[q], 1)
                    if old:
                        dve.wait_ge(idx_ready[p], pi + 2)
                        make_onehot(p, 0)
                        add(p, 3, pi, w, width)
                        for t in range(1, GROUP):
                            make_onehot(p, t)
                    messages(q, j, H2, C2, D)

            body2(2 * ITERS, True)
            with dve.Fori(2 * ITERS + 1, 3 * ITERS, 1) as i:
                body2(i, False)
            last_groups(3 * ITERS - 1, (ITERS - 1) * BODY, D + H2)
            pass_done(2)
            zv = heads[:, 0, 0:NB * H2].rearrange("p (w h) -> p w h", w=NB)
            by_head2 = tmp[:, :, :].rearrange("p w (h c) -> p w h c", h=H2)
            chain(v.tensor_scalar(zv, accv[:, :, D:D + H2], 1e-6, None, ALU.add))
            chain(v.reciprocal(zv, zv))
            chain(v.tensor_tensor(by_head2, accv[:, :, 0:D].rearrange("p w (h c) -> p w h c", h=H2), bc(zv, C2), ALU.mult))
            chain(v.tensor_tensor(xres[:, :, :], xres[:, :, :], tmp[:, :, :], ALU.add))
            norm("n3", xres[:, :, :], xres[:, :, :])

            ready("project3")
            for number, bias in ((3, "L3_gnn_b1"), (4, "L3_gnn_b2")):
                project(number, lambda b, p: v.tensor_scalar(
                    tab[:, bass.ds(b * D, D)], p[:, 0:D], dinv[:, bass.ds(b, 1)], None, ALU.mult))
                ready(f"table{number}")
                await_act(f"table{number}")
                linear_pass(number)
                chain(v.tensor_tensor(tmp[:, :, :], accv[:, :, 0:D], bc(dinv, D), ALU.mult))
                chain(v.tensor_tensor(tmp[:, :, :], tmp[:, :, :], mid(vrow[bias], NB), ALU.add))
                if number == 3:
                    ready("project4")
            chain(v.tensor_tensor(xres[:, :, :], xres[:, :, :], tmp[:, :, :], ALU.add))
            norm("n4", xres[:, :, :], xres[:, :, :], ("out0", "out1"))


LOADS = 15 + len(VECTORS)



def _norm(name):
    return [f"{name}_sq0", f"{name}_sq1", f"{name}_var"]


READY = {n: i + 1 for i, n in enumerate(
    ["project0", "table0", "gmax", "self", "pass0", *_norm("n0"), *_norm("n1"), "roots",
     "table1", "project1", *_norm("n2"),
     "project2", "table2", "pass2", *_norm("n3"),
     "project3", "table3", "project4", "table4", *_norm("n4"), "out0", "out1"])}
ACT_DONE = {n: i + 1 for i, n in enumerate(
    n for n in READY if n in ("self", "roots", "table3", "table4") or n.endswith(("_sq0", "_sq1", "_var")))}


EDGE_INS = {"src": 0, "dst": NO_NODE, "edge_attr_96": 0.0}


def kernel(**inputs):
    import numpy as _np
    import concourse.bacc as _bacc
    from concourse.bass_utils import run_bass_kernel_spmd as _run

    nc = _bacc.Bacc("TRN2", target_bir_lowering=False, num_devices=1)
    arrays, aps = {}, {}
    for name, a in inputs.items():
        a = _np.ascontiguousarray(a)
        if name in EDGE_INS:
            whole = _np.full((TILES * P,) + a.shape[1:], EDGE_INS[name], a.dtype)
            whole[:EDGES] = a
            a = whole
        arrays[f"in_{name}"] = a
        aps[name] = nc.dram_tensor(f"in_{name}", a.shape, mybir.dt.from_np(a.dtype), kind="ExternalInput").ap()
    out = nc.dram_tensor("out_x", (NODES, D), F32, kind="ExternalOutput").ap()
    gnn_stack(nc, aps, out)
    r = _run(nc, [arrays], core_ids=[0])
    return r.results[0]["out_x"]
```

```python
from contextlib import ExitStack

import concourse.bass as bass
from concourse import mybir

P = 128
NODES = 6250
EDGES = 200000
D = 96
NB = -(-NODES // P)
TAIL = NODES - (NB - 1) * P
GROUP = 4
GROUPS = 4
BODY = GROUP * GROUPS
EDGE_TILES = -(-EDGES // P)
STEPS = -(-(EDGE_TILES + NB - 1) // BODY) * BODY
ITERS = STEPS // BODY
TILES = STEPS
REACHED = STEPS - NB + 1
NSC = -(-STEPS // P)
TURNS = [(k, c, min(c + 4, NSC)) for k in range(4) for c in range(0, NSC, 4)]
PITCH = 104
H0, C0 = 4, 24
H2, C2 = 8, 12
PARTS0 = 3 * 2 * H0
T0 = D + H0
NO_NODE = 60000
PB = 7
PROJ_ITERS = NB // PB
TILE_ROWS = TILES // 16
E0, E1 = 1, GROUP - 1
BIG = 1000.0
SLOPE = 0.2
HUGE = 1e30
WINDOW = 60.0

F32 = mybir.dt.float32
BF16 = mybir.dt.bfloat16
I32 = mybir.dt.int32
ALU = mybir.AluOpType
ACT = mybir.ActivationFunctionType
AX = mybir.AxisListType.X
RMAX = bass.bass_isa.ReduceOp.max

VECTORS = ["L0_gnn_att_src", "L0_gnn_att_dst", "L0_gnn_bias", "L0_gnn_gamma", "L0_gnn_beta",
           "L3_gnn_b1", "L3_gnn_b2"]
OUT_PARTS = ((0, 10), (10, 28), (28, NB))
HALVES = ((0, NB // 2 + 1), (NB // 2 + 1, NB))

assert TILES % 16 == 0 and NSC <= 16 and PROJ_ITERS * PB == NB and TILES * P >= EDGES


def gnn_stack(nc, ins, out):
    with ExitStack() as ctx:
        def sb(name, shape, dt=F32):
            return ctx.enter_context(nc.sbuf_tensor(name, shape, dt))

        def sem(name):
            return ctx.enter_context(nc.semaphore(name))

        def sems(name, n):
            return [sem(f"{name}{i}") for i in range(n)]

        table = [nc.dram_tensor(f"table{i}", [NB * P, w], F32).ap() for i, w in enumerate([T0, D, 2 * D, D, D])]
        eproj = nc.dram_tensor("eproj", [TILES * P, D], F32).ap()
        row_dram = nc.dram_tensor("row_dram", [2, NSC * P], I32).ap()

        xres = sb("xres", [P, NB, D])
        acc = sb("acc", [P, NB * PITCH])
        qparts = [sb(f"qpart{i}", [P, NB * PITCH], BF16) for i in range(3)]
        qpart_v = [t[:, :].rearrange("p (w c) -> p w c", w=NB) for t in qparts]
        there = sb("there", [P, NB, 2 * H0])
        tab = sb("tab", [P, NB * 2 * D])
        tmp = sb("tmp", [P, NB, D])
        accv = acc[:, :].rearrange("p (w c) -> p w c", w=NB)
        tab96 = tab[:, 0:NB * D].rearrange("p (w c) -> p w c", w=NB)
        tab100 = tab[:, 0:NB * T0].rearrange("p (w c) -> p w c", w=NB)
        tab192 = tab[:, :].rearrange("p (w c) -> p w c", w=NB)
        node = sb("node", [P, 12, NB])
        heads = sb("heads", [P, 2, NB * H2])
        mean, var, std, rstd = (node[:, i, :] for i in range(4))
        in_deg, out_deg, ci, cj, dinv, lone, dtmp = (node[:, i, :] for i in range(4, 11))
        gmax = sb("gmax", [P, 2, H0])
        widest = sb("widest", [P, 2])
        far = sb("far", [1, 1], I32)

        WORDS = 3
        steps = sb("steps", [P, STEPS + BODY, WORDS], I32)
        src_s = steps[:, :, 0]
        drel_s, lo_s, hi_s = (steps[:, :, :].bitcast(BF16)[:, :, c] for c in (2, 3, 4))
        rows = sb("rows", [2, STEPS + BODY], I32)
        wrow, erow = rows[0:1, :], rows[1:2, :]
        ident = sb("ident", [P, P])
        ident_bf = sb("ident_bf", [P, P], BF16)
        iota = sb("iota", [P, P], BF16)
        iota_hi = sb("iota_hi", [P, NB])
        ones = sb("ones", [P, P])
        zero_bf = sb("zero_bf", [P, P], BF16)
        eps = sb("eps", [P, 1])
        w0 = sb("w0", [D, D + 2 * H0])
        w1 = sb("w1", [D + 1, D])
        wqkv = sb("wqkv", [D + 1, 3 * D])
        we = sb("we", [D + 1, D])
        w3a = sb("w3a", [D, D])
        w3b = sb("w3b", [D, D])
        vecs = sb("vecs", [P, len(VECTORS), D])
        vrow = {n: vecs[:, i, :] for i, n in enumerate(VECTORS)}

        cols = sb("cols", [P, GROUPS, GROUP, WORDS], I32)
        dcol, locol, hicol = (cols[:, :, :, :].bitcast(BF16)[:, :, :, c] for c in (2, 3, 4))
        gath = sb("gath", [P, BODY, 2 * D])
        onehot = sb("onehot", [P, GROUPS, GROUP, P], BF16)
        onehot_f = sb("onehot_f", [P, GROUPS, GROUP, P])
        onehot_t = sb("onehot_t", [P, GROUP, P], BF16)
        msg = sb("msg", [P, GROUPS, GROUP, PITCH])
        dvals = sb("dvals", [P, 2, GROUP, 2 * H0])
        logit = sb("logit", [P, 2, GROUP, H2])
        eattr = sb("eattr", [P, BODY, D])
        at = [NB * T0]

        def behind(n):
            at[0] += n
            return tab[:, at[0] - n:at[0]]

        src_lo = behind(GROUP * P).bitcast(BF16).rearrange("p (r j e) -> p r j e", r=2, j=GROUP)
        src_hi = behind(GROUP * NB).bitcast(BF16).rearrange("p (r j e) -> p r j e", r=2, j=GROUP)
        eout = behind(GROUPS * E1 * D).rearrange("p (q j c) -> p q j c", q=GROUPS, j=E1)
        eattr_t = behind(E1 * P)[0:D + 1, :].rearrange("p (j e) -> p j e", j=E1)
        prod = tab[:, 0:GROUP * D].rearrange("p (j c) -> p j c", j=GROUP)
        flat = gath[:, :, :].rearrange("p s c -> p (s c)")
        staged = flat[:, 0:PB * D].rearrange("p (b c) -> p b c", b=PB)
        xt = flat[0:D + 1, PB * D:PB * (D + P)].rearrange("p (b c) -> p b c", b=PB)

        ps = ctx.enter_context(nc.psum_tensor("ps", [P, 8, 512], F32))

        s_const = sem("s_const")
        s_load_dst = sem("s_load_dst")
        s_load = sem("s_load")
        s_rows = sems("s_rows", 2)
        s_wrap = sem("s_wrap")
        s_steps = sem("s_steps")
        s_eidx = sem("s_eidx")
        s_setup_pe = sem("s_setup_pe")
        s_setup_dve = sem("s_setup_dve")
        s_ready = sem("s_ready")
        s_table = sem("s_table")
        s_gmax = sem("s_gmax")
        s_far = sem("s_far")
        mx_cols, mx_gathered, mx_wide, mx_across, mx_chain = (
            sem(f"mx_{n}") for n in ("cols", "gathered", "wide", "across", "chain"))
        s_clear = sem("s_clear")
        s_act = sem("s_act")
        s_out = sem("s_out")
        chain_dve = sem("chain_dve")
        idx_ready = sems("idx_ready", GROUPS)
        onehot_ready = sems("onehot_ready", GROUPS)
        gathered = sems("gathered", GROUPS)
        summed = sems("summed", GROUPS)
        added = sems("added", GROUPS)
        turned = sems("turned", GROUPS)
        turned_sb = sems("turned_sb", GROUPS)
        spread = sems("spread", GROUPS)
        logits = sems("logits", GROUPS)
        exps = sems("exps", GROUPS)
        msgs = sems("msgs", GROUPS)
        histo = sems("histo", GROUPS)
        eloaded = sems("eloaded", GROUPS)
        onehot_f_ready = sems("onehot_f_ready", GROUPS)
        ein = sems("ein", GROUPS)
        eturned = sems("eturned", GROUPS)
        eturned_sb = sems("eturned_sb", GROUPS)
        eprojected = sems("eprojected", GROUPS)
        eout_ready = sems("eout_ready", GROUPS)
        estored = sems("estored", GROUPS)
        add_link = sems("add_link", BODY)
        link = [sems(f"link{q}_", 4) for q in range(GROUPS)]
        pool_step = sem("pool_step")
        proj_source = sem("proj_source")
        chunk_step = sem("chunk_step")
        proj_staged = sem("proj_staged")
        proj_turned = sems("proj_turned", 2)
        proj_sb = sems("proj_sb", 2)
        proj_done = sems("proj_done", PB)
        proj_out = sems("proj_out", PB)

        def bc(ap, n):
            return ap.unsqueeze(len(ap.shape)).broadcast_to(list(ap.shape) + [n])

        def mid(ap, n):
            return ap.unsqueeze(1).broadcast_to([ap.shape[0], n] + list(ap.shape[1:]))

        step_col = dtmp[:, 0:NSC]
        block_end = mean
        lmax = std[:, 0:16]
        tile_last = node[:, 11, :]
        advance = var
        wcol = rstd[:, 0:NSC]
        rows_cols = [heads[:, 0, 0:NSC].bitcast(I32), heads[:, 0, NSC:2 * NSC].bitcast(I32)]
        tile_idx = heads[:, 1, 0:NSC].bitcast(I32)
        ecol = heads[:, 1, NSC:2 * NSC]
        w128 = heads[:, 1, 2 * NSC:3 * NSC]
        cmp = tab[:, 0:NB * 16]
        steps_src, steps_dst = (tab[:, NB * T0 + i * NSC * P:NB * T0 + (i + 1) * NSC * P].rearrange(
            "p (c e) -> p c e", c=NSC).bitcast(I32) for i in range(2))
        int_lo = acc[:, 0:NSC * P].rearrange("p (c e) -> p c e", c=NSC).bitcast(I32)
        int_hi = acc[:, NSC * P:2 * NSC * P].rearrange("p (c e) -> p c e", c=NSC).bitcast(I32)
        f_src, f_dst = (part[:, 0:2 * NSC * P].bitcast(F32).rearrange("p (c e) -> p c e", c=NSC) for part in qparts[0:2])
        f_lo = tmp[:, :, :].rearrange("p a b -> p (a b)")[:, 0:NSC * P].rearrange("p (c e) -> p c e", c=NSC)
        f_hi = tmp[:, :, :].rearrange("p a b -> p (a b)")[:, NSC * P:2 * NSC * P].rearrange("p (c e) -> p c e", c=NSC)
        f_pen = acc[:, 2 * NSC * P:3 * NSC * P].rearrange("p (c e) -> p c e", c=NSC)

        mx_col = sb("mx_col", [P, 1, WORDS], I32)
        msg_flat = msg[:, :, :, :].rearrange("p q j c -> p (q j c)")
        mx_wide_sb = msg_flat[:, 0:H0 * P].rearrange("p (h e) -> p h e", h=H0)
        mx_masked_sb = msg_flat[:, H0 * P:2 * H0 * P].rearrange("p (h e) -> p h e", h=H0)
        mx_row_sb = msg_flat[:, 2 * H0 * P:2 * H0 * P + H0]
        mx_onehot_sb = qparts[1][:, 0:P]
        mx_mask_sb = qparts[2][:, 0:2 * P].bitcast(F32)

        def load_far(engine):
            return nc.values_load_multi_w_load_instructions(
                far[0:1, 0:1], engines=[engine], min_val=0, max_val=1,
                skip_runtime_bounds_check_because="a comparison's result")[1][0]

        def load_blocks(engine, s, n=GROUP):
            return nc.values_load_multi_w_load_instructions(
                wrow[0:1, bass.ds(s, n)], engines=[engine], min_val=0, max_val=(NB - 1) * PITCH,
                skip_runtime_bounds_check_because="the setup writes at most (NB - 1) * PITCH")[1]

        block = ctx.enter_context(nc.Block())

        @block.sync
        def _(sp):
            sp.dma_start(tmp[0:TILE_ROWS, 0:16 * P // D + 1, :].rearrange("p a b -> p (a b)")[:, 0:16 * P].bitcast(I32),
                         ins["dst"].rearrange("(p t) -> p t", p=TILE_ROWS)).then_inc(s_load_dst, 16)
            xv = ins["x"][0:(NB - 1) * P, :].rearrange("(w p) c -> p w c", p=P)
            sp.wait_ge(s_const, 1)
            sp.dma_start(xres[:, 0:NB - 1, :], xv).then_inc(s_load, 16)
            sp.dma_start(xres[0:TAIL, NB - 1, :], ins["x"][(NB - 1) * P:, :]).then_inc(s_load, 16)
            for t, n in ((w0, "L0_gnn_W"), (w1, "L1_gnn_weight"), (w3a, "L3_gnn_W1"), (w3b, "L3_gnn_W2"), (we, "L2_gnn_We")):
                sp.dma_start(t[0:D, 0:D], ins[n]).then_inc(s_load, 16)
            for i, n in enumerate("qkv"):
                sp.dma_start(wqkv[0:D, i * D:(i + 1) * D], ins[f"L2_gnn_W{n}"]).then_inc(s_load, 16)
                sp.dma_start(wqkv[D:D + 1, i * D:(i + 1) * D], ins[f"L2_gnn_b{n}"].rearrange("(a c) -> a c", a=1)).then_inc(s_load, 16)
            for t, n in ((w1, "L1_gnn_bias"), (we, "L2_gnn_be")):
                sp.dma_start(t[D:D + 1, :], ins[n].rearrange("(a c) -> a c", a=1)).then_inc(s_load, 16)
            for n in VECTORS:
                v = ins[n]
                v = v.rearrange("h c -> (h c)") if len(v.shape) == 2 else v
                sp.dma_start(vrow[n], v.partition_broadcast(P)).then_inc(s_load, 16)

            sp.wait_ge(s_eidx, 1)
            for i in range(2):
                sp.dma_start(row_dram[i, :].rearrange("(c p) -> p c", p=P), rows_cols[i],
                             allow_slow_non_contiguous=True).then_inc(s_rows[i], 16)
            for i, r in enumerate((wrow, erow)):
                sp.wait_ge(s_rows[i], 16)
                sp.dma_start(r[:, 0:STEPS], row_dram[i:i + 1, 0:STEPS]).then_inc(s_wrap, 16)
                sp.dma_start(r[:, STEPS:], row_dram[i:i + 1, 0:BODY]).then_inc(s_wrap, 16)

            def store_table(i, view):
                dram = table[i].rearrange("(w p) c -> p w c", p=P)
                for c in range(PROJ_ITERS):
                    sp.wait_ge(proj_out[PB - 1], i * PROJ_ITERS + c + 2)
                    sp.dma_start(dram[:, c * PB:(c + 1) * PB, :], view[:, c * PB:(c + 1) * PB, :]).then_inc(s_table, 16)

            attr = ins["edge_attr_96"].rearrange("(t p) c -> p t c", p=P)
            proj = eproj.rearrange("(t p) c -> p t c", p=P)

            def load_attributes(q, first, n):
                sp.dma_start(eattr[:, q * GROUP:q * GROUP + n, :], attr[:, bass.ds(first, n), :]).then_inc(ein[q], 16)

            def store_projected(q, i, first, n):
                sp.wait_ge(eout_ready[q], i)
                sp.dma_start(proj[:, bass.ds(first, n), :], eout[:, q, 0:n, :]).then_inc(estored[q], 16)

            for q in range(GROUPS):
                sp.sem_inc(estored[q], 16)
            store_table(0, tab100)
            for q in range(GROUPS):
                load_attributes(q, q * E0, E0)
            with sp.Fori(1, ITERS, 1) as i:
                for q in range(GROUPS):
                    sp.wait_ge(eturned[q], i)
                    load_attributes(q, (i * GROUPS + q) * E0, E0)
                    store_projected(q, i, (i * GROUPS - GROUPS + q) * E0, E0)
            base = ITERS * GROUPS * E0
            for q in range(GROUPS):
                sp.wait_ge(eturned[q], ITERS)
                load_attributes(q, base + q * E1, E1)
                store_projected(q, ITERS, base - (GROUPS - q) * E0, E0)
            for h, (a, b) in enumerate(HALVES):
                sp.wait_ge(s_ready, READY[f"table1_{h}"])
                sp.dma_start(table[1].rearrange("(w p) c -> p w c", p=P)[:, a:b, :], tab96[:, a:b, :]).then_inc(s_table, 16)
            with sp.Fori(1, ITERS, 1) as k:
                i = sp.snap(k + ITERS)
                for q in range(GROUPS):
                    sp.wait_ge(eturned[q], i)
                    load_attributes(q, (k * GROUPS + q) * E1 + base, E1)
                    store_projected(q, i, (k * GROUPS - GROUPS + q) * E1 + base, E1)
            for q in range(GROUPS):
                store_projected(q, 2 * ITERS, base + (ITERS * GROUPS - GROUPS + q) * E1, E1)
            for q in range(GROUPS):
                sp.wait_ge(estored[q], 2 * ITERS * 16 + 16)
            store_table(2, tab192)
            sp.wait_ge(s_wrap, 64)

            def load_projected(s, q):
                at = nc.values_load_multi_w_load_instructions(
                    erow[0:1, bass.ds(s + q * GROUP, GROUP)], engines=[mybir.EngineType.SP], min_val=0,
                    max_val=(REACHED - 1) * P, skip_runtime_bounds_check_because="the setup writes at most (REACHED - 1) * P")[1]
                for j in range(GROUP):
                    sp.dma_start(eattr[:, q * GROUP + j, :], eproj[bass.ds(at[j], P), :]).then_inc(
                        eloaded[q], 16)

            for q in range(GROUPS):
                load_projected(0, q)
            with sp.Fori(1, ITERS, 1) as k:
                for q in range(GROUPS):
                    sp.wait_ge(link[q][1], k + ITERS)
                    load_projected(k * BODY, q)
            store_table(3, tab96)
            store_table(4, tab96)
            for h, (a, b) in enumerate(OUT_PARTS):
                sp.wait_ge(s_ready, READY[f"out{h}"])
                z = min(b, NB - 1)
                sp.dma_start(out[a * P:z * P, :].rearrange("(w p) c -> p w c", p=P), xres[:, a:z, :]).then_inc(s_out, 16)
            sp.dma_start(out[(NB - 1) * P:, :], xres[0:TAIL, NB - 1, :]).then_inc(s_out, 16)
            sp.wait_ge(s_table, TABLE_STORED[-1])
            sp.wait_ge(s_out, 16 * (len(OUT_PARTS) + 1))

        @block.gpsimd
        def _(pool):
            g = nc.gpsimd
            g.memset(xres[:, NB - 1, :], 0.0).then_inc(s_const, 1)
            g.memset(ones[:, :], 1.0).then_inc(s_const, 1)
            g.memset(zero_bf[:, :], 0.0).then_inc(s_const, 1)
            g.memset(eps[:, :], 1e-5).then_inc(s_const, 1)
            g.iota(iota[:, :], [[1, P]], base=0, channel_multiplier=0, allow_small_or_imprecise_dtypes=True).then_inc(s_const, 1)
            g.iota(iota_hi[:, :], [[1, NB]], base=0, channel_multiplier=0, allow_small_or_imprecise_dtypes=True).then_inc(s_const, 1)
            g.iota(step_col, [[P, NSC]], base=0, channel_multiplier=1, allow_small_or_imprecise_dtypes=True).then_inc(s_const, 1)
            g.iota(block_end, [[P, NB]], base=P, channel_multiplier=0, allow_small_or_imprecise_dtypes=True).then_inc(s_const, 1)
            pool.wait_ge(s_const, 8)
            g.affine_select(out=ident[:, :], in_=ones[:, :], compare_op=ALU.is_equal, fill=0.0, base=0,
                            pattern=[[-1, P]], channel_multiplier=1).then_inc(s_const, 1)
            pool.wait_ge(s_const, 9)
            g.tensor_copy(ident_bf[:, :], ident[:, :]).then_inc(s_const, 1)
            g.memset(steps[:, :, :].bitcast(BF16)[:, :, 5], 0.0).then_inc(s_const, 1)
            pool.wait_ge(s_eidx, 1)
            for c in range(NSC):
                for arr, n in ((steps_src, "src"), (steps_dst, "dst")):
                    pool.indirect_dma_start(arr[:, c, :], None, ins[n].rearrange("(t e) -> t e", e=P),
                                            bass.IndirectOffsetOnAxis(ap=tile_idx[:, c:c + 1], axis=0)).then_inc(s_steps, 16)
            pool.wait_ge(s_ready, READY["gmax"])
            g.partition_all_reduce(gmax[:, 1, :], gmax[:, 0, :], P, RMAX).then_inc(s_gmax, 1)

            pool.wait_ge(s_ready, READY["widest"])
            g.partition_all_reduce(widest[:, 1:2], widest[:, 0:1], P, RMAX).then_inc(s_gmax, 1)
            pool.wait_ge(s_table, TABLE_STORED[0])
            pool.wait_ge(s_far, 1)
            with pool.If(load_far(mybir.EngineType.Pool) > 0):
                with pool.Fori(0, STEPS, 1) as s:
                    pool.wait_ge(mx_cols, s + 1)
                    pool.sem_inc(pool_step, 1)
                    pool.indirect_dma_start(gath[:, 0, 0:T0], None, table[0],
                                            bass.IndirectOffsetOnAxis(ap=mx_col[:, 0, 0:1], axis=0)).then_inc(mx_gathered, 16)
                pool.wait_ge(mx_chain, 4 * STEPS + 1)

            def gather_pass(number, width):
                pool.wait_ge(s_table, TABLE_STORED[number])
                with pool.Fori(number * ITERS, (number + 1) * ITERS, 1) as i:
                    for q in range(GROUPS):
                        pool.wait_ge(idx_ready[q], i + 1)
                        pool.sem_inc(pool_step, 1)
                        for j in range(GROUP):
                            slot = q * GROUP + j
                            pool.indirect_dma_start(
                                gath[:, slot, 0:width], None, table[number],
                                bass.IndirectOffsetOnAxis(ap=cols[:, q, j, 0:1], axis=0)).then_inc(gathered[q], 16)

            for number, width in enumerate([T0, D, 2 * D, D, D]):
                if number == 2:
                    pool.wait_ge(proj_source, PROJ_ITERS)
                    g.memset(acc[:, :], 0.0).then_inc(s_clear, 1)
                gather_pass(number, width)

        @block.tensor
        def _(pe):
            mm = nc.tensor.matmul
            pe.wait_ge(s_const, 10)
            pe.wait_ge(s_setup_dve, 1)
            mm(ps[:, 0, 0:NB], ones[0:TILE_ROWS, :], tile_last[0:TILE_ROWS, :], start=True, stop=True).then_inc(s_setup_pe, 1)

            def project(call, weights, width, k=D):
                with pe.Fori(call * PROJ_ITERS, (call + 1) * PROJ_ITERS, 1) as i:
                    pe.wait_ge(proj_staged, i + 1)
                    for half, blocks in enumerate((range(0, 4), range(4, PB))):
                        pe.wait_ge(proj_sb[half], i + 1)
                        for b in blocks:
                            t = nc.tensor.transpose(ps[0:D, half, b % 4 * P:b % 4 * P + P],
                                                    staged[:, b, :], ident[:, :])
                        t.then_inc(proj_turned[half], 1)
                    for b in range(PB):
                        if b % 4 == 0:
                            pe.wait_ge(proj_sb[b // 4], i + 2)
                        pe.wait_ge(proj_out[b], i + 1)
                        if b == 0:
                            pe.wait_ge(proj_out[PB - 1], i + 1)
                        if b == PB - 1:
                            pe.wait_ge(proj_out[0], i + 2)
                        mm(ps[:, 2 + b % 6, 0:width], xt[0:k, b, :], weights[0:k, 0:width],
                           start=True, stop=True).then_inc(proj_done[b], 1)

            project(0, w0, D + 2 * H0)
            pe.wait_ge(s_setup_dve, 2)
            for n, (k, c0, c1) in enumerate(TURNS):
                if n >= 8:
                    pe.wait_ge(s_setup_dve, 2 + n - 7)
                for c in range(c0, c1):
                    m = nc.tensor.transpose(ps[:, n % 8, (c - c0) * P:(c - c0 + 1) * P],
                                            (f_src, f_dst, f_lo, f_hi)[k][:, c, :], ident[:, :])
                m.then_inc(s_setup_pe, 1)

            def block_regs(s):
                return load_blocks(mybir.EngineType.PE, s)

            def turn(q, i, j):
                pe.wait_ge(onehot_ready[q], i + 1)
                for t in range(GROUP):
                    m = nc.tensor.transpose(ps[:, 0, :].bitcast(BF16)[:, t * P:t * P + P], onehot[:, q, t, :], ident_bf[:, :])
                m.then_inc(turned[q], 1)

            def spread_parts(q, j, s):
                w = block_regs(s)
                pe.wait_ge(turned_sb[q], j + 1)
                for t in range(GROUP):
                    m = mm(ps[:, 1 + q % 2, t * PARTS0:(t + 1) * PARTS0], onehot_t[:, t, :],
                           qparts[0][:, bass.ds(w[t], PARTS0)], start=True, stop=True)
                m.then_inc(spread[q], 1)

            def spread_rows(q, j, s):
                bank, width = 2 + q % 2, D
                w = block_regs(s)
                pe.wait_ge(turned_sb[q], j + 1)
                for t in range(GROUP):
                    for n, part in enumerate(qparts):
                        m = mm(ps[:, bank, t * width:(t + 1) * width], onehot_t[:, t, :], part[:, bass.ds(w[t], width)],
                               start=(n == 0), stop=(n == len(qparts) - 1))
                m.then_inc(spread[q], 1)

            def sums(q, i, width, source):
                pe.wait_ge(onehot_f_ready[q], i + 1)
                for t in range(GROUP):
                    m = mm(ps[:, 6 + q % 2, t * PITCH:t * PITCH + width], onehot_f[:, q, t, :], source(t),
                           start=True, stop=True)
                m.then_inc(summed[q], 1)

            def turn_attributes(q, i, n):
                pe.wait_ge(ein[q], i * 16 + 16)
                for t in range(n):
                    m = nc.tensor.transpose(ps[0:D, 4, t * P:t * P + P], eattr[:, q * GROUP + t, :], ident[:, :])
                m.then_inc(eturned[q], 1)

            def project_attributes(q, i, n):
                pe.wait_ge(eturned_sb[q], i + 1)
                for t in range(n):
                    m = mm(ps[:, 5, t * D:(t + 1) * D], eattr_t[:, t, :], we[:, :], start=True, stop=True)
                m.then_inc(eprojected[q], 1)

            pe.wait_ge(s_far, 1)
            with pe.If(load_far(mybir.EngineType.PE) > 0):
                with pe.Fori(0, STEPS, 1) as s:
                    pe.wait_ge(mx_wide, s + 1)
                    nc.tensor.transpose(ps[:, 0, :].bitcast(BF16)[:, 0:P], mx_onehot_sb, ident_bf[:, :])
                    for h in range(H0):
                        m = mm(ps[:, 1, h * P:(h + 1) * P], mx_wide_sb[:, h, :], ident[:, :], start=True, stop=True)
                    m.then_inc(mx_across, 1)

            pe.wait_ge(s_wrap, 64)
            pe.wait_ge(s_ready, READY["pass0"])
            mm(ps[:, 3, 0:NB], zero_bf[:, :], zero_bf[:, 0:NB], start=True, stop=False, skip_group_check=True)

            def count_sources(q, i):
                pe.wait_ge(histo[q], i + 1)
                for t in range(GROUP):
                    mm(ps[:, 3, 0:NB], src_lo[:, q % 2, t, :], src_hi[:, q % 2, t, :], start=False, stop=False,
                       skip_group_check=True)

            def slot0(q, i, last=False):
                b, ib = (q + 1, i) if q < 3 else (0, i + 1)
                c, ic = (q + 2, i) if q < 2 else (q - 2, i + 1)
                if not (last and q >= 2):
                    turn(c, ic, ic)
                count_sources(q, i)
                pe.wait_ge(msgs[q], i + 1)
                sums(q, i, D + H0 + 1, lambda t: msg[:, q, t, 0:D + H0 + 1])
                if not (last and q >= 2):
                    spread_parts(c, ic, ic * BODY + c * GROUP)
                project_attributes(q, i, E0)
                if not (last and q == 3):
                    turn_attributes(b, ib, E0)

            for q in (0, 1):
                turn(q, 0, 0)
                spread_parts(q, 0, q * GROUP)
            turn_attributes(0, 0, E0)
            with pe.Fori(0, ITERS - 1, 1) as i:
                for q in range(GROUPS):
                    slot0(q, i)
            for q in range(GROUPS):
                slot0(q, ITERS - 1, last=True)
            mm(ps[:, 3, 0:NB], zero_bf[:, :], zero_bf[:, 0:NB], start=False, stop=True,
               skip_group_check=True).then_inc(s_setup_pe, 1)

            def linear_pass(number, n):
                with pe.Fori(number * ITERS, (number + 1) * ITERS, 1) as i:
                    g = pe.snap((i + 1) * (16 * GROUP))
                    for q in range(GROUPS):
                        if n:
                            turn_attributes(q, i, n)
                        pe.wait_ge(onehot_f_ready[q], i + 1)
                        pe.wait_ge(added[(q + 2) % GROUPS], i + 1)
                        pe.wait_ge(gathered[q], g)
                        for t in range(GROUP):
                            m = mm(ps[:, 6 + q % 2, t * PITCH:t * PITCH + D], onehot_f[:, q, t, :],
                                   gath[:, q * GROUP + t, 0:D], start=True, stop=True)
                        m.then_inc(summed[q], 1)
                        if n:
                            project_attributes(q, i, n)

            linear_pass(1, E1)
            project(1, w1, D, D + 1)

            project(2, wqkv, 3 * D, D + 1)
            pe.wait_ge(s_ready, READY["pass2"])

            def slot2(q, i, j, now, last=False):
                n = 1 if q >= 2 else 0
                c = (q + 2) % GROUPS
                if not (last and q >= 2):
                    turn(c, i + n, j + n)
                pe.wait_ge(msgs[q], j + 1)
                sums(q, i, D + H2, lambda t: msg[:, q, t, 0:D + H2])
                if not (last and q >= 2):
                    spread_rows(c, j + n, now + n * BODY + c * GROUP)

            for q in (0, 1):
                turn(q, 2 * ITERS, ITERS)
                spread_rows(q, ITERS, q * GROUP)
            with pe.Fori(2 * ITERS, 3 * ITERS - 1, 1) as i:
                j = pe.snap(i - ITERS)
                now = pe.snap((i - 2 * ITERS) * BODY)
                for q in range(GROUPS):
                    slot2(q, i, j, now)
            for q in range(GROUPS):
                slot2(q, 3 * ITERS - 1, 2 * ITERS - 1, (ITERS - 1) * BODY, last=True)
            project(3, w3a, D)
            linear_pass(3, 0)
            project(4, w3b, D)
            linear_pass(4, 0)

        @block.scalar
        def _(act):
            for s in proj_sb:
                act.sem_inc(s, 1)
            act.wait_ge(s_const, 10)

            def project(call):
                if call == 0:
                    act.wait_ge(s_ready, READY["project0"])
                source = (xres, tmp, xres, xres, tmp)[call][:, :, :].rearrange("p w c -> p (w c)")
                with act.Fori(call * PROJ_ITERS, (call + 1) * PROJ_ITERS, 1) as i:
                    if call:
                        act.wait_ge(proj_source, i - (PROJ_ITERS - 1))
                    nc.scalar.activation(staged[:, :, :].rearrange("p b c -> p (b c)"),
                                         source[:, bass.ds((i - call * PROJ_ITERS) * PB * D, PB * D)],
                                         ACT.Relu if call == 4 else ACT.Copy).then_inc(proj_staged, 1)
                    for half, (a, b) in enumerate(((0, 4), (4, PB))):
                        act.wait_ge(proj_turned[half], i + 1)
                        nc.scalar.activation(xt[0:D, a:b, :], ps[0:D, half, 0:(b - a) * P].rearrange("p (b c) -> p b c", c=P),
                                             ACT.Copy).then_inc(proj_sb[half], 1)

            def whole(need, out_, in_, func, **kw):
                act.wait_ge(s_ready, READY[need])
                nc.scalar.activation(out_, in_, func, **kw).then_inc(s_act, 1)

            def norm_roots(name):
                for h, (a, b) in enumerate(HALVES):
                    whole(f"{name}_sq{h}", tab96[:, a:b, :], tmp[:, a:b, :], ACT.Square)
                whole(f"{name}_var", std, var, ACT.Sqrt, bias=eps[:, 0:1], scale=1.0 / D)

            def copy_turned(q, j):
                act.wait_ge(turned[q], j + 1)
                nc.scalar.activation(onehot_t[:, :, :], ps[:, 0, :].bitcast(BF16)[:, 0:GROUP * P].rearrange(
                    "p (j e) -> p j e", j=GROUP), ACT.Copy).then_inc(turned_sb[q], 1)

            def widen(q, i):
                act.wait_ge(onehot_ready[q], i + 1)
                nc.scalar.activation(onehot_f[:, q, :, :], onehot[:, q, :, :], ACT.Copy).then_inc(onehot_f_ready[q], 1)

            def exp_logits(q, j, heads_):
                act.wait_ge(logits[q], j + 1)
                nc.scalar.activation(msg[:, q, :, D:D + heads_], logit[:, q % 2, :, 0:heads_], ACT.Exp).then_inc(exps[q], 1)

            def copy_attributes(q, i, n):
                act.wait_ge(eturned[q], i + 1)
                nc.scalar.activation(eattr_t[0:D, 0:n, :], ps[0:D, 4, 0:n * P].rearrange("p (j e) -> p j e", j=n),
                                     ACT.Copy).then_inc(eturned_sb[q], 1)

            def copy_projected(q, i, n):
                act.wait_ge(eprojected[q], i + 1)
                act.wait_ge(estored[q], i * 16 + 16)
                nc.scalar.activation(eout[:, q, 0:n, :], ps[:, 5, 0:n * D].rearrange("p (j c) -> p j c", j=n),
                                     ACT.Copy).then_inc(eout_ready[q], 1)

            project(0)
            for name, to, of in (("step_src", f_src, steps_src), ("step_lo", f_lo, int_lo), ("step_hi", f_hi, int_hi)):
                whole(name, to, of, ACT.Copy)
            whole("self", accv[:, :, D:D + H0], accv[:, :, D:D + H0], ACT.Exp)

            def slot0(q, i, last=False):
                b, ib = (q + 1, i) if q < 3 else (0, i + 1)
                c, ic = (q + 2, i) if q < 2 else (q - 2, i + 1)
                if not (last and q >= 2):
                    copy_turned(c, ic)
                if not (last and q == 3):
                    exp_logits(b, ib, H0)
                if not (last and q >= 2):
                    widen(c, ic)
                copy_projected(q, i, E0)
                if not (last and q == 3):
                    copy_attributes(b, ib, E0)

            for q in (0, 1):
                copy_turned(q, 0)
            for q in (0, 1):
                widen(q, 0)
            exp_logits(0, 0, H0)
            copy_attributes(0, 0, E0)
            with act.Fori(0, ITERS - 1, 1) as i:
                for q in range(GROUPS):
                    slot0(q, i)
            for q in range(GROUPS):
                slot0(q, ITERS - 1, last=True)
            whole("roots", node[:, 6:9, :], node[:, 6:9, :], ACT.Sqrt)
            norm_roots("n0")
            norm_roots("n1")
            with act.Fori(ITERS, 2 * ITERS, 1) as i:
                for q in range(GROUPS):
                    widen(q, i)
                    if q:
                        copy_projected(q - 1, i, E1)
                    copy_attributes(q, i, E1)
                copy_projected(GROUPS - 1, i, E1)
            project(1)
            norm_roots("n2")
            project(2)
            for n in range(3):
                for h, (a, b) in enumerate(HALVES):
                    whole(f"q{n}_{h}", qpart_v[n][:, a:b, 0:D], tmp[:, a:b, :], ACT.Copy)

            def slot2(q, i, j, last=False):
                n = 1 if q >= 2 else 0
                c = (q + 2) % GROUPS
                if not (last and q >= 2):
                    copy_turned(c, j + n)
                if not (last and q == 3):
                    exp_logits((q + 1) % GROUPS, j + (1 if q == 3 else 0), H2)
                if not (last and q >= 2):
                    widen(c, i + n)

            for q in (0, 1):
                copy_turned(q, ITERS)
            for q in (0, 1):
                widen(q, 2 * ITERS)
            exp_logits(0, ITERS, H2)
            with act.Fori(ITERS, 2 * ITERS - 1, 1) as j:
                i = act.snap(j + ITERS)
                for q in range(GROUPS):
                    slot2(q, i, j)
            for q in range(GROUPS):
                slot2(q, 3 * ITERS - 1, 2 * ITERS - 1, last=True)
            norm_roots("n3")
            for number in (3, 4):
                project(number)
                whole(f"table{number}", accv[:, :, 0:D], tab96, ACT.Copy)
                with act.Fori(number * ITERS, (number + 1) * ITERS, 1) as i:
                    for q in range(GROUPS):
                        widen(q, i)
            norm_roots("n4")

        @block.vector
        def _(dve):
            v = nc.vector
            links = [0]
            told = [0]

            def chain(ins):
                links[0] += 1
                ins.then_inc(chain_dve, 1)
                dve.wait_ge(chain_dve, links[0])

            def ready(name):
                told[0] += 1
                assert READY[name] == told[0], name
                dve.sem_inc(s_ready, 1)

            def await_act(name):
                dve.wait_ge(s_act, ACT_DONE[name])

            def copy_columns(q, s):
                v.tensor_copy(cols[:, q, :, :], steps[:, bass.ds(s, GROUP), :]).then_inc(idx_ready[q], 1)

            def make_onehot(q, t):
                o = v.tensor_scalar(onehot[:, q, t, :], iota[:, :], dcol[:, q, t:t + 1], None, ALU.is_equal)
                if t == GROUP - 1:
                    o.then_inc(onehot_ready[q], 1)

            def turn_over(q, i, s, nxt):
                w = load_blocks(mybir.EngineType.DVE, s)
                dve.wait_ge(summed[q], i + 1)
                copy_columns(q, nxt)
                return w

            def add(q, t, i, w, width):
                if t:
                    dve.wait_ge(add_link[q * GROUP + t], i + 1)
                elif q:
                    dve.wait_ge(added[q - 1], i + (1 if q - 1 < 2 else 2))
                else:
                    dve.wait_ge(added[GROUPS - 1], i + 1)
                a = v.tensor_tensor(acc[:, bass.ds(w[t], width)], acc[:, bass.ds(w[t], width)],
                                    ps[:, 6 + q % 2, t * PITCH:t * PITCH + width], ALU.add)
                a.then_inc(added[q] if t == GROUP - 1 else add_link[q * GROUP + t + 1], 1)

            def add_and_refill(q, i, s, nxt, width):
                w = turn_over(q, i, s, nxt)
                for t in range(GROUP):
                    add(q, t, i, w, width)
                    if t == 0:
                        dve.wait_ge(idx_ready[q], i + 2)
                    make_onehot(q, t)

            def chunk(c):
                return bass.ds(c * PB, PB)

            def project(call, take, produce=None, after=None):
                def take_chunk(i, first):
                    for b in range(PB):
                        dve.wait_ge(proj_done[b], i + 1)
                        take(first + b, ps[:, 2 + b % 6, :]).then_inc(proj_out[b], 1)
                    if after:
                        for b in range(PB):
                            dve.wait_ge(proj_out[b], i + 2)
                        after(i - call * PROJ_ITERS).then_inc(chunk_step, 1)

                if produce:
                    produce(0).then_inc(proj_source, 1)
                with dve.Fori(call * PROJ_ITERS, (call + 1) * PROJ_ITERS - 1, 1) as i:
                    first = dve.snap(i * PB - call * NB)
                    if produce:
                        produce(i - (call * PROJ_ITERS - 1)).then_inc(proj_source, 1)
                    take_chunk(i, first)
                take_chunk((call + 1) * PROJ_ITERS - 1, NB - PB)
                for b in range(PB):
                    dve.wait_ge(proj_out[b], (call + 1) * PROJ_ITERS + 1)

            def norm(name, src, dst, parts=((0, NB),), summed=False):
                if not summed:
                    chain(v.tensor_reduce(mean, src, AX, ALU.add))
                chain(v.tensor_scalar(mean, mean, 1.0 / D, None, ALU.mult))
                for h, (a, b) in enumerate(HALVES):
                    chain(v.tensor_tensor(tmp[:, a:b, :], src[:, a:b, :], bc(mean[:, a:b], D), ALU.subtract))
                    ready(f"{name}_sq{h}")
                for h, (a, b) in enumerate(HALVES):
                    await_act(f"{name}_sq{h}")
                    chain(v.tensor_reduce(var[:, a:b], tab96[:, a:b, :], AX, ALU.add))
                ready(f"{name}_var")
                await_act(f"{name}_var")
                chain(v.reciprocal(rstd, std))
                if dst is None:
                    return
                for h, (a, b) in enumerate(parts):
                    chain(v.tensor_tensor(dst[:, a:b, :], tmp[:, a:b, :], bc(rstd[:, a:b], D), ALU.mult))
                    if parts == OUT_PARTS:
                        ready(f"out{h}")

            def split(x, parts):
                for n, part in enumerate(parts):
                    chain(v.tensor_copy(part, x))
                    if n < 2:
                        chain(v.tensor_tensor(x, x, part, ALU.subtract))

            xres_flat = xres[:, :, :].rearrange("p w c -> p (w c)")
            tmp_flat = tmp[:, :, :].rearrange("p w c -> p (w c)")

            def ones_row():
                chain(v.memset(xt[D:D + 1, :, :], 1.0))

            for s in (added[2], added[3], *proj_out):
                dve.sem_inc(s, 1)
            dve.wait_ge(s_const, 10)
            dve.wait_ge(s_load_dst, 16)
            R = TILE_ROWS
            edge_dst = tmp[0:R, :, :].rearrange("p a b -> p (a b)")[:, 0:16 * P].bitcast(I32)
            chain(v.tensor_reduce(lmax[0:R, :], edge_dst.rearrange("p (t e) -> p t e", e=P), AX, ALU.max))
            over = cmp[0:R, :].rearrange("p (w t) -> p w t", w=NB)
            chain(v.tensor_tensor(over, mid(lmax[0:R, :], NB), bc(block_end[0:R, :], 16), ALU.is_lt))
            chain(v.tensor_reduce(tile_last[0:R, :], over, AX, ALU.add))
            dve.sem_inc(s_setup_dve, 1)
            dve.wait_ge(s_setup_pe, 1)
            chain(v.tensor_tensor(advance, ps[:, 0, 0:NB], iota_hi[:, :], ALU.add))
            past = cmp[:, 0:NSC * (NB - 1)].rearrange("p (c w) -> p c w", c=NSC)
            chain(v.tensor_tensor(past, mid(advance[:, 0:NB - 1], NSC), bc(step_col, NB - 1), ALU.is_lt))
            chain(v.tensor_reduce(wcol, past, AX, ALU.add))
            chain(v.tensor_tensor(ecol, step_col, wcol, ALU.subtract))
            chain(v.tensor_scalar(ecol, ecol, float(REACHED - 1), None, ALU.min))
            chain(v.tensor_copy(tile_idx, ecol))
            chain(v.tensor_scalar(rows_cols[0], wcol, float(PITCH), None, ALU.mult))
            chain(v.tensor_scalar(rows_cols[1], ecol, float(P), None, ALU.mult))
            chain(v.tensor_scalar(w128, wcol, float(P), None, ALU.mult))
            dve.sem_inc(s_eidx, 1)

            dve.wait_ge(s_load, 16 * LOADS)
            for at_, att in ((D, "L0_gnn_att_src"), (T0, "L0_gnn_att_dst")):
                chain(v.tensor_tensor(eattr[0:D, 0, :], w0[:, 0:D], vrow[att][0:D, :], ALU.mult))
                chain(v.tensor_reduce(w0[:, at_:at_ + H0], eattr[0:D, 0, :].rearrange("p (h c) -> p h c", h=H0), AX, ALU.add))
            ready("project0")
            there_flat = there[:, :, :].rearrange("p w c -> p (w c)")

            def take0(b, p):
                v.tensor_copy(tab[:, bass.ds(b * T0, T0)], p[:, 0:T0])
                return v.tensor_copy(there_flat[:, bass.ds(b * (2 * H0), H0)], p[:, T0:T0 + H0])

            project(0, take0)
            a_src, a_dst, guard = tab100[:, :, D:T0], there[:, :, 0:H0], there[:, :, H0:]
            chain(v.tensor_reduce(gmax[:, 0, :], a_src.rearrange("p w h -> p h w"), AX, ALU.max))
            ready("gmax")
            bound = node[:, 4:8, :].rearrange("p k w -> p (k w)").rearrange("p (w h) -> p w h", h=H0)
            self_logit = guard

            def leaky(x):
                return v.scalar_tensor_tensor(out=x, in0=x, scalar=SLOPE, in1=x, op0=ALU.mult, op1=ALU.max)

            chain(v.tensor_tensor(self_logit, a_src, a_dst, ALU.add))
            chain(leaky(self_logit))
            dve.wait_ge(s_gmax, 1)
            chain(v.tensor_tensor(bound, a_dst, mid(gmax[:, 1, :], NB), ALU.add))
            chain(leaky(bound))
            above = qparts[2][:, 0:2 * NB * H0].bitcast(F32).rearrange("p (w h) -> p w h", h=H0)
            chain(v.tensor_tensor(above, bound, self_logit, ALU.subtract))
            chain(v.tensor_reduce(widest[:, 0:1], qparts[2][:, 0:2 * NB * H0].bitcast(F32), AX, ALU.max))
            ready("widest")
            dve.wait_ge(s_gmax, 2)
            chain(v.tensor_scalar(far[0:1, 0:1], widest[0:1, 1:2], WINDOW, None, ALU.is_gt))
            dve.sem_inc(s_far, 1)

            dve.wait_ge(s_steps, 16 * 2 * NSC)
            ready("step_src")
            chain(v.tensor_scalar(int_lo, steps_src, P - 1, None, ALU.bitwise_and))
            ready("step_lo")
            chain(v.tensor_scalar(int_hi, steps_src, P.bit_length() - 1, None, ALU.logical_shift_right))
            ready("step_hi")
            chain(v.tensor_copy(f_dst, steps_dst))
            chain(v.tensor_tensor(f_dst, f_dst, bc(w128, P), ALU.subtract))
            chain(v.tensor_scalar(f_pen, f_dst, float(P - 1), BIG, ALU.subtract, ALU.mult))
            await_act("step_hi")
            chain(v.tensor_tensor(f_hi, f_hi, f_pen, ALU.max))
            chain(v.scalar_tensor_tensor(out=f_hi, in0=f_dst, scalar=-BIG, in1=f_hi, op0=ALU.mult, op1=ALU.max))
            dve.sem_inc(s_setup_dve, 1)
            chain(v.memset(eattr_t[D:D + 1, :, :], 1.0))
            dve.wait_ge(s_const, 11)
            for n, (k, c0, c1) in enumerate(TURNS):
                m = min(c1 * P, STEPS) - c0 * P
                dve.wait_ge(s_setup_pe, 2 + n)
                v.tensor_copy((src_s, drel_s, lo_s, hi_s)[k][:, c0 * P:c0 * P + m], ps[:, n % 8, 0:m]).then_inc(s_setup_dve, 1)
            dve.wait_ge(s_setup_dve, 2 + len(TURNS))
            chain(v.tensor_copy(steps[:, STEPS:, :], steps[:, 0:BODY, :]))
            for q in range(GROUPS):
                copy_columns(q, q * GROUP)
                dve.wait_ge(idx_ready[q], 1)
                for t in range(GROUP):
                    make_onehot(q, t)
            dve.wait_ge(s_wrap, 64)

            htab = tab100[:, :, 0:D]
            by_head = tmp[:, :, :].rearrange("p w (h c) -> p w h c", h=H0)
            hv = heads[:, 0, 0:NB * H0].rearrange("p (w h) -> p w h", w=NB)
            ex_self = accv[:, :, D:D + H0]
            with dve.If(load_far(mybir.EngineType.DVE) > 0):
                v.memset(acc[:, :], -HUGE).then_inc(mx_chain, 1)
                with dve.Fori(0, STEPS, 1) as s:
                    done = dve.snap(s * 4)
                    w = load_blocks(mybir.EngineType.DVE, s, 1)[0]
                    dve.wait_ge(mx_chain, done + 1)
                    v.tensor_copy(mx_col[:, :, :], steps[:, bass.ds(s, 1), :]).then_inc(mx_cols, 1)
                    dve.wait_ge(mx_cols, s + 1)
                    v.tensor_scalar(mx_onehot_sb, iota[:, :], mx_col[:, :, :].bitcast(BF16)[:, 0, 2:3], None,
                                    ALU.is_equal)
                    dve.wait_ge(mx_gathered, (s + 1) * 16)
                    v.tensor_copy(mx_wide_sb, bc(gath[:, 0, D:T0], P)).then_inc(mx_wide, 1)
                    dve.wait_ge(mx_across, s + 1)
                    v.tensor_scalar(mx_mask_sb, ps[:, 0, :].bitcast(BF16)[:, 0:P], 1.0, HUGE,
                                    ALU.subtract, ALU.mult).then_inc(mx_chain, 1)
                    dve.wait_ge(mx_chain, done + 2)
                    v.tensor_tensor(mx_masked_sb, ps[:, 1, 0:H0 * P].rearrange("p (h e) -> p h e", h=H0),
                                    mid(mx_mask_sb, H0), ALU.add).then_inc(mx_chain, 1)
                    dve.wait_ge(mx_chain, done + 3)
                    v.tensor_reduce(mx_row_sb, mx_masked_sb, AX, ALU.max).then_inc(mx_chain, 1)
                    dve.wait_ge(mx_chain, done + 4)
                    v.tensor_tensor(acc[:, bass.ds(w, H0)], acc[:, bass.ds(w, H0)], mx_row_sb, ALU.max).then_inc(mx_chain, 1)
                dve.wait_ge(mx_chain, 4 * STEPS + 1)
                v.tensor_tensor(bound, accv[:, :, 0:H0], a_dst, ALU.add).then_inc(mx_chain, 1)
                dve.wait_ge(mx_chain, 4 * STEPS + 2)
                leaky(bound).then_inc(mx_chain, 1)
                dve.wait_ge(mx_chain, 4 * STEPS + 3)
            chain(v.memset(msg[:, :, :, D + H0:D + H0 + 1], 1.0))
            chain(v.scalar_tensor_tensor(out=hv, in0=bound, scalar=-WINDOW, in1=self_logit, op0=ALU.add, op1=ALU.max))
            chain(v.tensor_tensor(ex_self, self_logit, hv, ALU.subtract))
            chain(v.tensor_copy(guard, hv))
            ready("self")
            await_act("self")
            chain(v.tensor_tensor(accv[:, :, 0:D].rearrange("p w (h c) -> p w h c", h=H0),
                                  htab.rearrange("p w (h c) -> p w h c", h=H0), bc(ex_self, C0), ALU.mult))
            chain(v.memset(accv[:, :, D + H0:D + H0 + 1], 0.0))
            split(there[:, :, :], [qpart_v[0][:, :, n * 2 * H0:(n + 1) * 2 * H0] for n in range(3)])
            ready("pass0")

            def messages(q, j, h, c, at):
                dve.wait_ge(exps[q], j + 1)
                v.tensor_tensor(msg[:, q, :, 0:D].rearrange("p j (h c) -> p j h c", h=h),
                                gath[:, q * GROUP:(q + 1) * GROUP, at:at + D].rearrange("p j (h c) -> p j h c", h=h),
                                bc(msg[:, q, :, D:D + h], c), ALU.mult).then_inc(msgs[q], 1)

            def body0(i, first):
                g = (i + 1) * (16 * GROUP) if first else dve.snap((i + 1) * (16 * GROUP))
                now = i * BODY if first else dve.snap(i * BODY)
                prev = None if first else dve.snap(i - 1)
                for q in range(GROUPS):
                    p = (q + 2) % GROUPS
                    pi, ps_, pn = (i, now, now + BODY) if q >= 2 else (prev, now - BODY if not first else None, now)
                    old = q >= 2 or not first
                    width = D + H0 + 1
                    if old:
                        w = turn_over(p, pi, ps_ + p * GROUP, pn + p * GROUP)
                    dve.wait_ge(gathered[q], g)
                    dve.wait_ge(spread[q], i + 1)
                    parts = ps[:, 1 + q % 2, 0:GROUP * PARTS0].rearrange("p (j k c) -> p j c k", j=GROUP, k=3)
                    dst = dvals[:, q % 2, :, :]
                    v.tensor_reduce(dst, parts, AX, ALU.add).then_inc(link[q][0], 1)
                    if old:
                        dve.wait_ge(idx_ready[p], pi + 2)
                        make_onehot(p, 0)
                    dve.wait_ge(link[q][0], i + 1)
                    lg = logit[:, q % 2, :, 0:H0]
                    v.tensor_tensor(lg, gath[:, q * GROUP:(q + 1) * GROUP, D:D + H0], dst[:, :, 0:H0], ALU.add).then_inc(link[q][1], 1)
                    if old:
                        add(p, 0, pi, w, width)
                    dve.wait_ge(link[q][1], i + 1)
                    v.scalar_tensor_tensor(out=lg, in0=lg, scalar=SLOPE, in1=lg, op0=ALU.mult, op1=ALU.max).then_inc(link[q][2], 1)
                    if old:
                        make_onehot(p, 1)
                    dve.wait_ge(link[q][2], i + 1)
                    v.tensor_tensor(lg, lg, dst[:, :, H0:2 * H0], ALU.subtract).then_inc(link[q][3], 1)
                    if old:
                        add(p, 1, pi, w, width)
                    dve.wait_ge(link[q][3], i + 1)
                    v.tensor_scalar(lg, lg, WINDOW, None, ALU.min).then_inc(logits[q], 1)
                    for t in range(GROUP):
                        v.tensor_scalar(src_lo[:, q % 2, t, :], iota[:, :], locol[:, q, t:t + 1], None, ALU.is_equal)
                        if old and t % 2 == 0:
                            make_onehot(p, 2 + t // 2)
                            add(p, 2 + t // 2, pi, w, width)
                    v.tensor_tensor(src_hi[:, q % 2, :, :], mid(iota_hi[:, :], GROUP),
                                    bc(hicol[:, q, :], NB), ALU.is_equal).then_inc(histo[q], 1)
                    messages(q, i, H0, C0, 0)

            def last_groups(i, now, width):
                for q in (2, 3):
                    add_and_refill(q, i, now + q * GROUP, now + BODY + q * GROUP, width)

            body0(0, True)
            chain(v.tensor_tensor(tab96, xres[:, :, :], mid(vrow["L0_gnn_bias"], NB), ALU.add))
            with dve.Fori(1, ITERS, 1) as i:
                body0(i, False)
            last_groups(ITERS - 1, (ITERS - 1) * BODY, D + H0 + 1)

            def pass_done(number):
                dve.wait_ge(added[GROUPS - 1], (number + 1) * ITERS + 1)

            pass_done(0)
            dve.wait_ge(s_setup_pe, 2 + len(TURNS))
            chain(v.tensor_copy(in_deg, accv[:, :, D + H0]))
            chain(v.tensor_copy(out_deg, ps[:, 3, 0:NB]))
            chain(v.tensor_scalar(ci, out_deg, 1.0, None, ALU.max))
            chain(v.tensor_scalar(cj, in_deg, 1.0, None, ALU.max))
            chain(v.tensor_scalar(dinv, in_deg, 1.0, None, ALU.add))
            chain(v.tensor_scalar(lone, in_deg, 0.0, None, ALU.is_equal))
            ready("roots")
            chain(v.tensor_scalar(hv, ex_self, 1e-16, None, ALU.add))
            chain(v.reciprocal(hv, hv))
            chain(v.tensor_tensor(by_head, accv[:, :, 0:D].rearrange("p w (h c) -> p w h c", h=H0), bc(hv, C0), ALU.mult))
            chain(v.tensor_tensor(tmp[:, :, :], tmp[:, :, :], tab96, ALU.add))
            norm("n0", tmp[:, :, :], tmp[:, :, :])
            chain(v.tensor_tensor(tmp[:, :, :], tmp[:, :, :], mid(vrow["L0_gnn_gamma"], NB), ALU.mult))
            chain(v.tensor_tensor(tmp[:, :, :], tmp[:, :, :], mid(vrow["L0_gnn_beta"], NB), ALU.add))
            chain(v.scalar_tensor_tensor(out=xres[:, :, :], in0=tmp[:, :, :], scalar=0.0, in1=xres[:, :, :], op0=ALU.max, op1=ALU.add))
            norm("n1", xres[:, :, :], None)

            def linear_pass(number):
                with dve.Fori(number * ITERS, (number + 1) * ITERS, 1) as i:
                    now = dve.snap((i - number * ITERS) * BODY)
                    nxt = dve.snap(now + BODY)
                    for q in range(GROUPS):
                        add_and_refill(q, i, now + q * GROUP, nxt + q * GROUP, D)
                pass_done(number)

            await_act("roots")
            chain(v.reciprocal(node[:, 6:9, :], node[:, 6:9, :]))
            chain(v.tensor_tensor(dtmp, rstd, ci, ALU.mult))
            for h, (a, b) in enumerate(HALVES):
                chain(v.tensor_tensor(tab96[:, a:b, :], tmp[:, a:b, :], bc(dtmp[:, a:b], D), ALU.mult))
                ready(f"table1_{h}")
            chain(v.tensor_tensor(xres[:, :, :], tmp[:, :, :], bc(rstd, D), ALU.mult))
            chain(v.tensor_tensor(accv[:, :, 0:D], xres[:, :, :], bc(lone, D), ALU.mult))
            linear_pass(1)
            ones_row()
            project(1, lambda b, p: v.tensor_tensor(
                        xres_flat[:, bass.ds(b * D, D)], xres_flat[:, bass.ds(b * D, D)], p[:, 0:D], ALU.add),
                    lambda c: v.tensor_tensor(tmp[:, chunk(c), :], accv[:, chunk(c), 0:D], bc(cj[:, chunk(c)], D), ALU.mult),
                    lambda c: v.tensor_reduce(mean[:, chunk(c)], xres[:, chunk(c), :], AX, ALU.add))
            dve.wait_ge(chunk_step, PROJ_ITERS)
            norm("n2", xres[:, :, :], None, summed=True)

            def normed(c):
                return v.tensor_tensor(xres[:, chunk(c), :], tmp[:, chunk(c), :], bc(rstd[:, chunk(c)], D), ALU.mult)

            for q in range(GROUPS):
                dve.wait_ge(estored[q], 2 * ITERS * 16 + 16)

            def take2(b, p):
                v.tensor_copy(tab[:, bass.ds(b * (2 * D), 2 * D)], p[:, D:3 * D])
                return v.tensor_scalar(tmp_flat[:, bass.ds(b * D, D)], p[:, 0:D], float(C2) ** -0.5, None, ALU.mult)

            project(2, take2, normed)
            for h in range(2):
                ready(f"q0_{h}")
            for n in range(2):
                for h, (a, b) in enumerate(HALVES):
                    await_act(f"q{n}_{h}")
                    chain(v.tensor_tensor(tmp[:, a:b, :], tmp[:, a:b, :], qpart_v[n][:, a:b, 0:D], ALU.subtract))
                    ready(f"q{n + 1}_{h}")
            await_act("q2_1")
            dve.wait_ge(s_clear, 1)
            ready("pass2")

            def body2(i, first):
                keep = (lambda x: x) if first else dve.snap
                j = keep(i - ITERS)
                g = keep((i + 1) * (16 * GROUP))
                e = keep((i - 2 * ITERS + 1) * (16 * GROUP))
                now = keep((i - 2 * ITERS) * BODY)
                prev = None if first else dve.snap(i - 1)
                width = D + H2
                for q in range(GROUPS):
                    p = (q + 2) % GROUPS
                    pi, ps_, pn = (i, now, now + BODY) if q >= 2 else (prev, now - BODY if not first else None, now)
                    old = q >= 2 or not first
                    if old:
                        w = turn_over(p, pi, ps_ + p * GROUP, pn + p * GROUP)
                    dve.wait_ge(gathered[q], g)
                    dve.wait_ge(spread[q], j + 1)
                    at_dst = ps[:, 2 + q % 2, 0:GROUP * D].rearrange("p (j c) -> p j c", j=GROUP)
                    v.tensor_tensor(prod[:, :, :], gath[:, q * GROUP:(q + 1) * GROUP, 0:D], at_dst, ALU.mult).then_inc(link[q][0], 1)
                    if old:
                        add(p, 0, pi, w, width)
                    dve.wait_ge(eloaded[q], e)
                    dve.wait_ge(link[q][0], j + 1)
                    v.tensor_tensor(prod[:, :, :], prod[:, :, :], eattr[:, q * GROUP:(q + 1) * GROUP, :], ALU.mult).then_inc(link[q][1], 1)
                    if old:
                        add(p, 1, pi, w, width)
                    dve.wait_ge(link[q][1], j + 1)
                    lg = logit[:, q % 2, :, 0:H2]
                    v.tensor_reduce(lg, prod[:, :, :].rearrange("p j (h c) -> p j h c", h=H2), AX, ALU.add).then_inc(link[q][2], 1)
                    if old:
                        add(p, 2, pi, w, width)
                    dve.wait_ge(link[q][2], j + 1)
                    v.tensor_scalar(lg, lg, 5.0, -5.0, ALU.min, ALU.max).then_inc(logits[q], 1)
                    if old:
                        dve.wait_ge(idx_ready[p], pi + 2)
                        make_onehot(p, 0)
                        add(p, 3, pi, w, width)
                        for t in range(1, GROUP):
                            make_onehot(p, t)
                    messages(q, j, H2, C2, D)

            body2(2 * ITERS, True)
            with dve.Fori(2 * ITERS + 1, 3 * ITERS, 1) as i:
                body2(i, False)
            last_groups(3 * ITERS - 1, (ITERS - 1) * BODY, D + H2)
            pass_done(2)
            zv = heads[:, 0, 0:NB * H2].rearrange("p (w h) -> p w h", w=NB)
            by_head2 = tmp[:, :, :].rearrange("p w (h c) -> p w h c", h=H2)
            chain(v.tensor_scalar(zv, accv[:, :, D:D + H2], 1e-6, None, ALU.add))
            chain(v.reciprocal(zv, zv))
            chain(v.tensor_tensor(by_head2, accv[:, :, 0:D].rearrange("p w (h c) -> p w h c", h=H2), bc(zv, C2), ALU.mult))
            chain(v.tensor_tensor(xres[:, :, :], xres[:, :, :], tmp[:, :, :], ALU.add))
            norm("n3", xres[:, :, :], None)

            def hidden(c):
                v.tensor_tensor(tmp[:, chunk(c), :], accv[:, chunk(c), 0:D], bc(dinv[:, chunk(c)], D), ALU.mult).then_inc(chunk_step, 1)
                dve.wait_ge(chunk_step, c + PROJ_ITERS + 1)
                return v.tensor_tensor(tmp[:, chunk(c), :], tmp[:, chunk(c), :], mid(vrow["L3_gnn_b1"], PB), ALU.add)

            for number, source in ((3, normed), (4, hidden)):
                project(number, lambda b, p: v.tensor_scalar(
                    tab[:, bass.ds(b * D, D)], p[:, 0:D], dinv[:, bass.ds(b, 1)], None, ALU.mult), source)
                ready(f"table{number}")
                await_act(f"table{number}")
                if number == 4:
                    chain(v.tensor_tensor(xres[:, :, :], xres[:, :, :], mid(vrow["L3_gnn_b2"], NB), ALU.add))
                linear_pass(number)
            chain(v.tensor_tensor(tmp[:, :, :], accv[:, :, 0:D], bc(dinv, D), ALU.mult))
            chain(v.tensor_tensor(xres[:, :, :], xres[:, :, :], tmp[:, :, :], ALU.add))
            norm("n4", xres[:, :, :], xres[:, :, :], OUT_PARTS)


LOADS = 15 + len(VECTORS)


def _norm(name):
    return [f"{name}_sq0", f"{name}_sq1", f"{name}_var"]


READY = {n: i + 1 for i, n in enumerate(
    ["project0", "gmax", "widest", "step_src", "step_lo", "step_hi", "self", "pass0", "roots", *_norm("n0"), *_norm("n1"),
     "table1_0", "table1_1", *_norm("n2"),
     *(f"q{n}_{h}" for n in range(3) for h in range(2)), "pass2", *_norm("n3"),
     "table3", "table4", *_norm("n4"), *(f"out{h}" for h in range(len(OUT_PARTS)))])}
ACT_DONE = {n: i + 1 for i, n in enumerate(
    n for n in READY if n in ("step_src", "step_lo", "step_hi", "self", "roots", "table3", "table4")
    or n.endswith(("_sq0", "_sq1", "_var")) or n[0] == "q")}


TABLE_STORED = [16 * sum((PROJ_ITERS, len(HALVES), PROJ_ITERS, PROJ_ITERS, PROJ_ITERS)[:i + 1]) for i in range(5)]


EDGE_INS = {"src": 0, "dst": NO_NODE, "edge_attr_96": 0.0}


def kernel(**inputs):
    import numpy as _np
    import concourse.bacc as _bacc
    from concourse.bass_utils import run_bass_kernel_spmd as _run

    nc = _bacc.Bacc("TRN2", target_bir_lowering=False, num_devices=1)
    arrays, aps = {}, {}
    for name, a in inputs.items():
        a = _np.ascontiguousarray(a)
        if name in EDGE_INS:
            whole = _np.full((TILES * P,) + a.shape[1:], EDGE_INS[name], a.dtype)
            whole[:EDGES] = a
            a = whole
        arrays[f"in_{name}"] = a
        aps[name] = nc.dram_tensor(f"in_{name}", a.shape, mybir.dt.from_np(a.dtype), kind="ExternalInput").ap()
    out = nc.dram_tensor("out_x", (NODES, D), F32, kind="ExternalOutput").ap()
    gnn_stack(nc, aps, out)
    r = _run(nc, [arrays], core_ids=[0])
    return r.results[0]["out_x"]
```
